# Optimizing a Trainium2 kernel written in Bass

```python
import numpy as np
import jax
import jax.numpy as jnp

def _softmax(x, axis=-1):
    return jax.nn.softmax(x, axis=axis)

def _gelu(x):
    return jax.nn.gelu(x, approximate=True)

def _silu(x):
    return jax.nn.silu(x)

def _sigmoid(x):
    return jax.nn.sigmoid(x)

def _layernorm(x, axis=-1, eps=1e-05):
    m = jnp.mean(x, axis=axis, keepdims=True)
    v = jnp.var(x, axis=axis, keepdims=True)
    return (x - m) / jnp.sqrt(v + eps)

def _scatter_add(tgt, idx, src, axis=0):
    return tgt.at[idx].add(src)

def _segment_sum(src, seg, n):
    return jax.ops.segment_sum(src, seg, n)
kernel_name = 'mk_adaln_d1_jaxref_r4_8c4e5a'

def setup_inputs(seed: int=0):
    np.random.seed(seed)
    _w = jnp.asarray

    def _L0_attn_setup():
        import jax, jax.numpy as jnp
        import numpy as np
        B, S, D, H, WIN = (2, 512, 256, 16, 128)
        DK = D // H
        NEG_INF = float('-inf')

        def _sliding_window_softmax(scores):
            b, h, s, _ = scores.shape
            nb = s // WIN
            causal = jnp.tril(jnp.ones((s, s), dtype=bool)).reshape(1, 1, nb, WIN, nb, WIN)
            sc = scores.reshape(b, h, nb, WIN, nb, WIN)
            sc = jnp.where(causal, sc, NEG_INF)
            m = jnp.max(sc, axis=-1, keepdims=True)
            e = jnp.exp(sc - jnp.where(jnp.isfinite(m), m, 0.0))
            e = jnp.where(causal, e, 0.0)
            denom = jnp.sum(e, axis=-1, keepdims=True)
            probs = e / jnp.where(denom == 0.0, 1.0, denom)
            return probs.reshape(b, h, s, s)
        key = jax.random.key(seed)
        ks = jax.random.split(key, 9)
        sc = 1.0 / np.sqrt(D)

        def w(k):
            return jax.random.normal(k, (D, D), jnp.float32) * sc

        def b(k):
            return jax.random.normal(k, (D,), jnp.float32) * 0.01
        return {'x': jax.random.normal(ks[0], (B, S, D), jnp.float32), 'Wq_w': w(ks[1]), 'Wq_b': b(jax.random.fold_in(ks[1], 1)), 'Wk_w': w(ks[2]), 'Wk_b': b(jax.random.fold_in(ks[2], 1)), 'Wv_w': w(ks[3]), 'Wv_b': b(jax.random.fold_in(ks[3], 1)), 'Wo_w': w(ks[4]), 'Wo_b': b(jax.random.fold_in(ks[4], 1))}
    _L0_attn_in = _L0_attn_setup()

    def _L0_ffn_setup():
        import jax, jax.numpy as jnp
        import numpy as np
        import math
        BETA = 0.9
        THRESHOLD = 1.0
        NUM_STEPS = 5
        ALPHA = 2.0

        @jax.custom_vjp
        def spike_fn(u):
            return (u > 0).astype(u.dtype)

        def _spike_fwd(u):
            return (spike_fn(u), u)

        def _spike_bwd(u, g):
            s = jnp.pi / 2.0 * ALPHA * u
            return (g * (ALPHA / 2.0) / (1.0 + s * s),)
        spike_fn.defvjp(_spike_fwd, _spike_bwd)
        key = jax.random.key(seed)
        k1, k2, k3 = jax.random.split(key, 3)
        n_embd = 256
        x = jax.random.normal(k1, (4, 512, n_embd), dtype=jnp.float32)
        W_fc = jax.random.normal(k2, (4 * n_embd, n_embd), dtype=jnp.float32) / math.sqrt(n_embd)
        W_proj = jax.random.normal(k3, (n_embd, 4 * n_embd), dtype=jnp.float32) / math.sqrt(4 * n_embd)
        return {'x': x, 'W_fc': W_fc, 'W_proj': W_proj}
    _L0_ffn_in = _L0_ffn_setup()
    _L0_c = _w((lambda *s: np.random.randn(*s).astype(np.float32) * 0.05)(8, 256))
    _L0_wmod = _w((lambda *s: np.random.randn(*s).astype(np.float32) * 0.05)(256, 6 * 256) * 256 ** (-0.5))
    _d = {'L0_attn_x': _L0_attn_in['x'], 'L0_attn_Wq_w': _L0_attn_in['Wq_w'], 'L0_attn_Wq_b': _L0_attn_in['Wq_b'], 'L0_attn_Wk_w': _L0_attn_in['Wk_w'], 'L0_attn_Wk_b': _L0_attn_in['Wk_b'], 'L0_attn_Wv_w': _L0_attn_in['Wv_w'], 'L0_attn_Wv_b': _L0_attn_in['Wv_b'], 'L0_attn_Wo_w': _L0_attn_in['Wo_w'], 'L0_attn_Wo_b': _L0_attn_in['Wo_b'], 'L0_ffn_W_fc': _L0_ffn_in['W_fc'], 'L0_ffn_W_proj': _L0_ffn_in['W_proj'], 'L0_c': _L0_c, 'L0_wmod': _L0_wmod}
    _x0 = _d['L0_attn_x']
    _d['L0_attn_x'] = jax.random.normal(jax.random.fold_in(jax.random.key(seed), 1), (8, 1024, 256), dtype=_x0.dtype)
    del _x0
    return _d

def reference(L0_attn_x, L0_attn_Wq_w, L0_attn_Wq_b, L0_attn_Wk_w, L0_attn_Wk_b, L0_attn_Wv_w, L0_attn_Wv_b, L0_attn_Wo_w, L0_attn_Wo_b, L0_ffn_W_fc, L0_ffn_W_proj, L0_c, L0_wmod):

    def _L0_attn_ref(x, Wq_w, Wq_b, Wk_w, Wk_b, Wv_w, Wv_b, Wo_w, Wo_b):
        import jax, jax.numpy as jnp
        import numpy as np
        B, S, D, H, WIN = (2, 512, 256, 16, 128)
        DK = D // H
        NEG_INF = float('-inf')

        def _sliding_window_softmax(scores):
            b, h, s, _ = scores.shape
            nb = s // WIN
            causal = jnp.tril(jnp.ones((s, s), dtype=bool)).reshape(1, 1, nb, WIN, nb, WIN)
            sc = scores.reshape(b, h, nb, WIN, nb, WIN)
            sc = jnp.where(causal, sc, NEG_INF)
            m = jnp.max(sc, axis=-1, keepdims=True)
            e = jnp.exp(sc - jnp.where(jnp.isfinite(m), m, 0.0))
            e = jnp.where(causal, e, 0.0)
            denom = jnp.sum(e, axis=-1, keepdims=True)
            probs = e / jnp.where(denom == 0.0, 1.0, denom)
            return probs.reshape(b, h, s, s)
        b, s, d = x.shape
        q = (x @ Wq_w.T + Wq_b).reshape(b, s, H, DK).transpose(0, 2, 1, 3)
        k = (x @ Wk_w.T + Wk_b).reshape(b, s, H, DK).transpose(0, 2, 1, 3)
        v = (x @ Wv_w.T + Wv_b).reshape(b, s, H, DK).transpose(0, 2, 1, 3)
        attn_scores = jnp.einsum('bhqd,bhkd->bhqk', q, k) / np.sqrt(DK)
        if WIN < s:
            attn_scores = _sliding_window_softmax(attn_scores)
        attn_probs = jax.nn.softmax(attn_scores, axis=-1)
        attn_out = jnp.einsum('bhqk,bhkd->bhqd', attn_probs, v)
        attn_out = attn_out.transpose(0, 2, 1, 3).reshape(b, s, d)
        return attn_out @ Wo_w.T + Wo_b

    def _L0_ffn_ref(x, W_fc, W_proj):
        import jax, jax.numpy as jnp
        import numpy as np
        import math
        BETA = 0.9
        THRESHOLD = 1.0
        NUM_STEPS = 5
        ALPHA = 2.0

        @jax.custom_vjp
        def spike_fn(u):
            return (u > 0).astype(u.dtype)

        def _spike_fwd(u):
            return (spike_fn(u), u)

        def _spike_bwd(u, g):
            s = jnp.pi / 2.0 * ALPHA * u
            return (g * (ALPHA / 2.0) / (1.0 + s * s),)
        spike_fn.defvjp(_spike_fwd, _spike_bwd)
        h = jnp.square(jax.nn.relu(jnp.einsum('bsd,fd->bsf', x, W_fc)))
        y = jnp.einsum('bsf,df->bsd', h, W_proj)

        def step(mem, _):
            reset = jax.lax.stop_gradient(spike_fn(mem - THRESHOLD))
            mem_new = BETA * mem + y - reset * THRESHOLD
            spk = spike_fn(mem_new - THRESHOLD)
            return (mem_new, spk)
        mem0 = jnp.zeros_like(y)
        _, spks = jax.lax.scan(step, mem0, None, length=NUM_STEPS)
        return jnp.sum(spks, axis=0) / NUM_STEPS
    x = L0_attn_x
    mod = (_silu(L0_c) @ L0_wmod).reshape(L0_c.shape[0], 6, 1, -1)
    sa, ca, ga, sb, cb, gb = (mod[:, 0], mod[:, 1], mod[:, 2], mod[:, 3], mod[:, 4], mod[:, 5])
    ga = (2 * (ga >= 0) - 1) * jnp.maximum(jnp.abs(ga), 0.25)
    gb = (2 * (gb >= 0) - 1) * jnp.maximum(jnp.abs(gb), 0.25)
    h = _layernorm(x, axis=-1) * (1 + ca) + sa
    x = x + ga * _L0_attn_ref(h, L0_attn_Wq_w, L0_attn_Wq_b, L0_attn_Wk_w, L0_attn_Wk_b, L0_attn_Wv_w, L0_attn_Wv_b, L0_attn_Wo_w, L0_attn_Wo_b)
    h = _layernorm(x, axis=-1) * (1 + cb) + sb
    x = x + gb * _L0_ffn_ref(h, L0_ffn_W_fc, L0_ffn_W_proj)
    return x

_drawn_inputs = setup_inputs


def setup_inputs(seed=0):
    import zlib

    import numpy as np

    out = dict(_drawn_inputs(seed))
    spreads = {}
    factors = {'L0_attn_Wq_w': 8.0,
     'L0_attn_Wq_b': 64.0,
     'L0_attn_Wk_w': 8.0,
     'L0_attn_Wk_b': 64.0,
     'L0_attn_Wv_w': 6.143,
     'L0_attn_Wv_b': 8.0,
     'L0_attn_Wo_w': 6.157,
     'L0_attn_Wo_b': 23.235}
    for name, (base, spread) in spreads.items():
        noise = np.random.default_rng([zlib.crc32(name.encode()), seed]).standard_normal(out[name].shape)
        drawn = base * np.exp(spread * noise) if base else spread * noise
        out[name] = jnp.asarray(drawn.astype(out[name].dtype))
    for name, factor in factors.items():
        out[name] = (out[name] * factor).astype(out[name].dtype)
    return out
```

```python
from contextlib import ExitStack

import concourse.bass as bass
from concourse import mybir

F32 = mybir.dt.float32
BF16 = mybir.dt.bfloat16
ACT = mybir.ActivationFunctionType
ALU = mybir.AluOpType
AX_X = mybir.AxisListType.X

B, S, D, H, DK = 8, 1024, 256, 16, 16
FF = 4 * D
P = 128
NB = S // P
NT = D // P
NF = FF // P
QH = 4
NQ = H // QH
BANK = 512
EPS = 1e-5
MASKED = -1e30

QP = [0, 0, 0, 1, 1, 2]
KP = [0, 1, 2, 0, 1, 0]
KROWS = DK * len(QP)
VW = 32
ST_PARTS = 3

UNITS = [
    [(0, 0, 512)],
    [(1, 128, 512), (3, 384, 512)],
    [(2, 256, 512), (6, 768, 1024)],
    [(0, 512, 1024)],
    [(1, 512, 1024)],
    [(2, 512, 1024)],
    [(3, 512, 1024)],
    [(4, 512, 1024)],
    [(5, 640, 1024), (7, 896, 1024)],
]
NU = len(UNITS)
A_UNITS = 3
TILES = [[(7, 0)], [(6, 0), (0, 896)], [(5, 0), (1, 768)], [(4, 0), (2, 640)], [(3, 0)]]
NTILE = len(TILES)
SLOTS = 8 * NTILE
SLOT_OF = {i: 8 * t + off // P for t, tile in enumerate(TILES) for i, off in tile}
RING_HEAD = NTILE + 1
RING_S = QH * RING_HEAD
RING_R = NU * QH // 2


def columns(u):
    out, at = [], 0
    for strip in UNITS[u]:
        out.append((strip, at))
        at += strip[2] - strip[1]
    return out


def ring_order():
    out = []
    for hh in range(QH):
        for t in range(NTILE):
            out.append(("s", hh, t))
            if t == 1 and hh:
                out.append(("m", hh - 1, 0))
    return out + [("m", QH - 1, 0)]


RING = ring_order()
RING_AT = {use: n for n, use in enumerate(RING)}

USE_HT1, USE_QK, USE_V, USE_SUF = 0, 4, 12, 16
USE_AT, USE_O, USE_HT2, USE_F1, USE_F2 = 17, 21, 25, 29, 45
USES = 49

PER = {
    "x_loaded": 16, "mod_loaded": 32, "ln_stats": 2, "ln_aggr": 2, "ln_log": 2, "ln_exp": 2,
    "ln_newton": 8, "xn_ready": 16, "dense_ready": USES, "dense_evac": USES, "split": 16,
    "stored0": 32, "stored1": 32, "stack0": 384, "stack1": 384, "ring_ready": NQ * (RING_S + RING_R),
    "ring_free": NQ * (RING_S + RING_R), "max_hi": H, "max_lo": H, "st_ready": NQ * NU * QH,
    "e1_done": NQ * NU * QH, "d_ready": 2 * NQ, "r_log": 2 * NQ, "r_exp": 2 * NQ, "r_newton": 4 * NQ,
    "r_hi": 2 * NQ, "r_rest": 2 * NQ, "r_mid": 2 * NQ, "rp_ready": 2 * NQ, "e2_done": NQ * RING_R,
    "pv_ready": NQ, "pv_evac": NQ, "ot_ready": NQ, "o_rec": NQ, "o_norm": NQ, "v_ready": 1,
    "xres_ready": 3, "ao": 4, "x2_ready": 4, "sq_done": 16, "lif": 52, "fin": 8, "out_stored": 64,
}

C_ID, C_MQ, C_MT, C_SEL, C_DS, C_U, C_SA, C_OH, C_AB = 0, 128, 256, 384, 416, 672, 736, 864, 1888
C_END = 1890


def constants():
    import numpy as np

    c = np.zeros((P, C_END), np.float32)
    r = np.arange(P)
    c[:, C_ID:C_ID + P] = np.eye(P)
    c[:, C_MQ:C_MQ + P] = MASKED * (r[None, :] > r[:, None])
    c[:, C_MT:C_MT + P] = MASKED * (r[:, None] > r[None, :])
    for hh in range(QH):
        for j in range(NB):
            for part in range(ST_PARTS):
                c[32 * hh + 8 * part + j, C_SEL + NB * hh + j] = -1.0
    for j in range(NB):
        for part in range(ST_PARTS):
            c[:, C_DS + 32 * j + 8 * part + j] = 1.0
        c[:, C_U + NB * j:C_U + NB * j + j] = 1.0
    for i in range(NB):
        c[i, C_SA:C_SA + P] = (r % 32 >= 8 * ST_PARTS) | (r % 8 > i)
        for row in (i, KROWS + 2 * i, KROWS + 2 * i + 1):
            c[row, C_OH + P * i:C_OH + P * (i + 1)] = 1.0
    c[:, C_AB] = -1.0 * (r % 32 >= 8)
    c[:, C_AB + 1] = -1.0 * (r % 32 >= 16)
    return c


def build(nc, x, wqT, wkT, wvT, woT, bq, bk, bv, bo, wfcT, wprojT, cT, wmod, consts, out):
    mod_dram = nc.dram_tensor("mod_scratch", (B, 6 * D), F32).ap()
    part_dram = [nc.dram_tensor(f"{n}_parts", (3, D, S), BF16).ap() for n in "qk"]

    with ExitStack() as ctx:
        def sb(name, shape, dt=F32):
            return ctx.enter_context(nc.sbuf_tensor(name, shape, dt))

        def sem(name):
            return ctx.enter_context(nc.semaphore(name))

        x_res = sb("x_res", [P, NB, D])
        tok = sb("tok", [P, NB, D])
        hT = sb("hT", [P, NT, S])
        q_st = sb("q_st", [P, 2, QH, S], BF16)
        k_st = sb("k_st", [P, 2, QH, S], BF16)
        v1 = sb("v1", [P, NB, H, VW])
        e = sb("e", [P, QH, NU * BANK])
        ef = e[:, :, :].rearrange("p h n -> p (h n)")
        qk_f = ef[:, 0:4 * S].rearrange("p (t n) -> p t n", t=4)
        qk_p = ef[:, 4 * S:10 * S].bitcast(BF16).rearrange("p (t a n) -> p t a n", t=4, a=3)
        gT = ef[:, 0:NF * S].rearrange("p (f n) -> p f n", f=NF)
        n1 = ef[:, 8 * S:10 * S]
        neg = ef[:, 10 * S:12 * S]
        lin = ef[:, 12 * S:14 * S]
        acc = ef[:, 14 * S:16 * S]
        x_in = ef[:, 16 * S:18 * S]
        w_q, w_k, w_v, w_o = (sb(n, [P, NT, D]) for n in ("w_q", "w_k", "w_v", "w_o"))
        w_fc = sb("w_fc", [P, NT, FF])
        w_proj = sb("w_proj", [P, NF, D])
        b_qk = sb("b_qk", [P, 2, NT])
        b_v = sb("b_v", [P, D])
        b_o = sb("b_o", [P, D])
        modc = sb("modc", [P, 6 * NT])
        gates = sb("gates", [P, 2, D])
        bo_g = sb("bo_g", [P, D])
        gb5 = sb("gb5", [P, D])
        r_a = sb("r_a", [P, S])
        r_b = sb("r_b", [P, S])
        r_h = sb("r_h", [P, S], BF16)
        r_p = sb("r_p", [P, S], BF16)
        o_t = sb("o_t", [P, S])
        suf = sb("suf", [P, NQ, NB])
        o_rcp = sb("o_rcp", [P, NB * QH])
        negmax = sb("negmax", [P, 2, SLOTS])
        maxp = sb("maxp", [P, 2, SLOTS, 2], BF16)
        stats = sb("stats", [P, NB, 6])
        mv = sb("mv", [P, NB, 2])
        rstd = sb("rstd", [P, NB])
        ln_a = sb("ln_a", [P, NB])
        ln_b = sb("ln_b", [P, NB])
        eps = sb("eps", [P, 1])
        ab = sb("ab", [P, 2])
        id_f = sb("id_f", [P, P])
        id_b = sb("id_b", [P, P], BF16)
        mask_q = sb("mask_q", [P, P], BF16)
        mask_t = sb("mask_t", [P, P], BF16)
        sel = sb("sel", [P, QH * NB, P], BF16)
        d_ones = sb("d_ones", [P, NB, 32])
        u_ind = sb("u_ind", [P, NB, NB])
        seed_a = sb("seed_a", [P, P], BF16)
        seed_b = sb("seed_b", [P, S], BF16)
        c_sb = ef[:, 0:C_END]
        wmod_sb = ef[:, 4 * S:4 * S + NT * 6 * D].rearrange("p (k n) -> p k n", k=NT)
        c_T = ef[:, 8 * S:8 * S + NT * B]
        c_e = ef[:, 9 * S:9 * S + NT * B]
        c_s = ef[:, 10 * S:10 * S + NT * B]
        mod_sb = ef[0:B, 12 * S:12 * S + 6 * D]
        mod_t = ef[0:B, 14 * S:14 * S + 2 * D]
        mod_u = ef[0:B, 14 * S + 2 * D:14 * S + 4 * D]

        ring = [ctx.enter_context(nc.psum_tensor(f"ring{i}", [P, 2 * BANK], F32)) for i in range(2)]
        st = ctx.enter_context(nc.psum_tensor("st", [P, 2 * BANK], F32))
        dd = ctx.enter_context(nc.psum_tensor("dd", [P, 2 * BANK], F32))

        def bank(i):
            t = [ring[0], ring[1], st, dd][i % 8 // 2]
            return t[:, BANK * (i % 2):BANK * (i % 2) + BANK]

        s = {n: sem(n) for n in PER}
        weights_in, consts_in, ready, mod_step = (
            sem(n) for n in ("weights_in", "consts_in", "ready", "mod_step"))
        s_modmm = sem("mod_product")
        mod_own = sem("mod_own")

        def val(b, name, n):
            return b * PER[name] + n

        def strip_e(u, hh, c, strip):
            at = BANK * u + c
            return e[:, hh, at:at + strip[2] - strip[1]]

        block = ctx.enter_context(nc.Block())

        @block.sync
        def _(sp):
            sp.dma_start(c_sb, consts).then_inc(consts_in, 16)
            sp.dma_start(c_T, cT).then_inc(consts_in, 16)
            sp.dma_start(wmod_sb, wmod.rearrange("(k p) n -> p k n", p=P)).then_inc(consts_in, 16)
            for t, w in ((w_q, wqT), (w_k, wkT), (w_v, wvT), (w_o, woT), (w_fc, wfcT), (w_proj, wprojT)):
                sp.dma_start(t[:, :, :], w.rearrange("(k p) n -> p k n", p=P)).then_inc(weights_in, 16)
            for n, v in enumerate((bq, bk)):
                sp.dma_start(b_qk[:, n, :], v).then_inc(weights_in, 16)
            for t, v in ((b_v, bv), (b_o, bo)):
                sp.dma_start(t[:, :], v.rearrange("(a n) -> a n", a=1).to_broadcast([P, D])).then_inc(weights_in, 16)
            sp.wait_ge(mod_step, 9)
            sp.dma_start(mod_dram, mod_sb).then_inc(s["out_stored"], 16)
            sp.wait_ge(s["out_stored"], 16)
            sp.wait_ge(ready, 1)
            x_rows = x.rearrange("b (t p) d -> p b t d", p=P)
            o_rows = out.rearrange("b (t p) d -> p b t d", p=P)
            sp.dma_start(x_in.rearrange("p (b t d) -> p b t d", b=1, t=NB), x_rows[:, 0:1, :, :]).then_inc(s["x_loaded"], 16)
            with sp.Fori(0, B) as b:
                b_next = sp.snap((b + 1) % B)
                sp.dma_start(modc[:, :].rearrange("p (b n) -> p b n", b=1),
                             mod_dram.rearrange("b (n p) -> p b n", p=P)[:, bass.ds(b, 1), :],
                             allow_slow_non_contiguous=True).then_inc(s["mod_loaded"], 16)
                sp.dma_start(gates[:, :, :],
                             mod_dram.rearrange("b (a c n) -> b a c n", a=2, c=3)[bass.ds(b, 1), :, 2, :]
                             .to_broadcast([P, 2, D])).then_inc(s["mod_loaded"], 16)
                for ot in range(NT):
                    for t in range(2):
                        sp.wait_ge(s["split"], val(b, "split", 4 * (2 * ot + t) + 4))
                        sp.dma_start(part_dram[t][:, P * ot:P * ot + P, :].rearrange("a p n -> p a n"),
                                     qk_p[:, 2 * ot + t, :, :]).then_inc(s[f"stored{ot}"], 16)

                def stacks(g):
                    if g >= 2:
                        scored = sp.snap(val(b, "st_ready", NU * QH * (g - 1)))
                    if g % 2 == 0:
                        sp.wait_ge(s[f"stored{g // 2}"], val(b, f"stored{g // 2}", 32))
                    if g >= 2:
                        sp.wait_ge(s["st_ready"], scored)
                    f0 = QH * DK * g
                    for stack, parts, dram in ((q_st, QP, part_dram[0]), (k_st, KP, part_dram[1])):
                        for n, a in enumerate(parts):
                            sp.dma_start(stack[DK * n:DK * n + DK, g % 2, :, :],
                                         dram[a, f0:f0 + QH * DK, :].rearrange("(h d) n -> d h n", h=QH),
                                         ).then_inc(s[f"stack{g % 2}"], 16)

                for g in range(NQ):
                    stacks(g)
                sp.wait_ge(s["pv_ready"], val(b, "pv_ready", NQ))
                sp.dma_start(x_in.rearrange("p (b t d) -> p b t d", b=1, t=NB),
                             x_rows[:, bass.ds(b_next, 1), :, :]).then_inc(s["x_loaded"], 16)
                for c in range(4):
                    sp.wait_ge(s["fin"], val(b, "fin", 2 * c + 2))
                    sp.dma_start(o_rows[:, bass.ds(b, 1), 2 * c:2 * c + 2, :],
                                 acc[:, BANK * c:BANK * c + BANK].rearrange("p (b t d) -> p b t d", b=1, t=2),
                                 ).then_inc(s["out_stored"], 16)
            sp.wait_ge(s["out_stored"], 16 + B * PER["out_stored"])
            sp.wait_ge(s["x_loaded"], (B + 1) * 16)

        @block.tensor
        def _(pe):
            pe.wait_ge(consts_in, 48)
            pe.wait_ge(mod_step, 3)
            for n in range(3):
                for k in range(NT):
                    mm = pe.matmul(bank(n)[0:B, :], c_s[:, B * k:B * k + B], wmod_sb[:, k, BANK * n:BANK * n + BANK],
                                   start=(k == 0), stop=(k == NT - 1))
            mm.then_inc(s_modmm, 1)
            pe.wait_ge(weights_in, 160)
            pe.wait_ge(ready, 2)

            with pe.Fori(0, B) as b:

                def take(use):
                    if use >= 8:
                        pe.wait_ge(s["dense_evac"], val(b, "dense_evac", use - 7))
                    return bank(use)

                def turn(use0, xn0):
                    for half in range(2):
                        for ft in range(NT):
                            ps = take(use0 + NT * half + ft)
                            if xn0 is not None:
                                pe.wait_ge(s["xn_ready"], val(b, "xn_ready", xn0 + 4 * half + 4))
                            for n in range(4):
                                mm = pe.transpose(ps[:, P * n:P * n + P], tok[:, 4 * half + n, P * ft:P * ft + P], id_f[:, :])
                            mm.then_inc(s["dense_ready"], 1)

                turn(USE_HT1, 0)
                for ot in range(NT):
                    for t, w in enumerate((w_q, w_k)):
                        for half in range(2):
                            use = USE_QK + 4 * ot + 2 * t + half
                            ps = take(use)
                            if ot == 0 and t == 0:
                                pe.wait_ge(s["dense_evac"], val(b, "dense_evac", USE_HT1 + 2 * half + 2))
                            for k in range(NT):
                                mm = pe.matmul(ps, w[:, k, P * ot:P * ot + P], hT[:, k, BANK * half:BANK * half + BANK],
                                               start=(k == 0), stop=(k == NT - 1))
                            mm.then_inc(s["dense_ready"], 1)
                for n in range(4):
                    ps = take(USE_V + n)
                    for i in range(2):
                        for k in range(NT):
                            mm = pe.matmul(ps[:, D * i:D * i + D], hT[:, k, P * (2 * n + i):P * (2 * n + i) + P], w_v[:, k, :],
                                           start=(k == 0), stop=(k == NT - 1))
                    mm.then_inc(s["dense_ready"], 1)
                ps = take(USE_SUF)
                pe.wait_ge(s["v_ready"], val(b, "v_ready", 1))
                for g in range(NQ):
                    for j in range(1, NB):
                        mm = pe.matmul(ps[:, NB * g:NB * g + NB], v1[:, j, QH * g:QH * g + QH, :].rearrange("p h c -> p (h c)"),
                                       u_ind[:, j, :], start=(j == 1), stop=(j == NB - 1))
                mm.then_inc(s["dense_ready"], 1)

                def ring_use(g, n, r):
                    kind, hh, t = RING[n]
                    par = g % 2
                    slot = ring[r % 2]
                    if r >= 2:
                        pe.wait_ge(s["ring_free"], val(b, "ring_free", r - 1))
                    if n == 0:
                        pe.wait_ge(s[f"stack{par}"], val(b, f"stack{par}", 192 * (g // 2 + 1)))
                    if kind == "s":
                        for i, off in TILES[t]:
                            q = q_st[0:KROWS, par, hh, P * i:P * i + P]
                            c, end, diag = off, off + P * (i + 1), off + P * i
                            while c < end:
                                stop = min(end, (c // BANK + 1) * BANK)
                                last = c <= diag < stop
                                mm = pe.matmul(slot[:, c:stop], q, k_st[0:KROWS, par, hh, c - off:stop - off],
                                               start=True, stop=not last, skip_group_check=True)
                                if last:
                                    mm = pe.matmul(slot[:, diag:diag + P], id_b[:, :], mask_q[:, :],
                                                   start=False, stop=True, skip_group_check=True)
                                c = stop
                    else:
                        pe.wait_ge(s["max_lo"], val(b, "max_lo", QH * g + hh + 1))
                        view = slot[:, 0:BANK].bitcast(BF16)
                        for i in range(NB):
                            at = SLOT_OF[i]
                            mm = pe.transpose(view[KROWS:KROWS + 16, P * i:P * i + P], maxp[:, hh % 2, at:at + NB, :].rearrange("p w a -> p (w a)"), id_b[:, :])
                    mm.then_inc(s["ring_ready"], 1)

                def sums(g, u):
                    pe.wait_ge(s["e1_done"], val(b, "e1_done", QH * (NU * g + u + 1)))
                    for strip, c in columns(u):
                        for hh in range(QH):
                            mm = pe.matmul(dd[32 * hh:32 * hh + 32, strip[1]:strip[2]], d_ones[:, strip[0], :], strip_e(u, hh, c, strip),
                                           start=False, stop=False, skip_group_check=True)
                    if u in (A_UNITS - 1, NU - 1):
                        mm.then_inc(s["d_ready"], 1)

                def outputs(g):
                    pe.wait_ge(s["pv_evac"], val(b, "pv_evac", g + 1))
                    for i in range(NB):
                        mm = pe.transpose(dd[:, P * i:P * i + P], o_t[:, P * i:P * i + P], id_f[:, :])
                    mm.then_inc(s["ot_ready"], 1)

                pe.wait_ge(s["dense_evac"], val(b, "dense_evac", USE_SUF + 1))
                for n in range(RING_S):
                    ring_use(0, n, n)
                for g in range(NQ):
                    r0 = RING_S + g * (RING_S + RING_R)
                    used = 0
                    for u in range(NU + 2):
                        if u < NU:
                            if g + 1 < NQ:
                                while used < RING_S * (u + 1) // NU:
                                    ring_use(g + 1, used, r0 + used)
                                    used += 1
                            for hh in range(QH):
                                n = QH * (NU * g + u) + hh
                                slot = st[:, BANK * (n % 2):BANK * (n % 2) + BANK]
                                if n % (NU * QH) < 2:
                                    if g:
                                        pe.wait_ge(s["pv_evac"], val(b, "pv_evac", g))
                                else:
                                    pe.wait_ge(s["e1_done"], val(b, "e1_done", n - 1))
                                if u == 0:
                                    base = (g * (RING_S + RING_R) - RING_R) if g else 0
                                    pe.wait_ge(s["ring_free"], val(b, "ring_free", base + RING_AT[("m", hh, 0)] + 1))
                                for (j, qa, qb), c in columns(u):
                                    diag = qa == P * j
                                    mm = pe.matmul(slot[:, c:c + qb - qa], k_st[:, g % 2, hh, P * j:P * j + P], q_st[:, g % 2, hh, qa:qb],
                                                   start=True, stop=not diag, skip_group_check=True)
                                    if diag:
                                        mm = pe.matmul(slot[:, c:c + P], id_b[:, :], mask_t[:, :],
                                                       start=False, stop=True, skip_group_check=True)
                                mm.then_inc(s["st_ready"], 1)
                        if u == 1 and g:
                            outputs(g - 1)
                        if u == 2:
                            if g:
                                pe.wait_ge(s["o_norm"], val(b, "o_norm", g))
                            for half in range(2):
                                pe.matmul(dd[:, BANK * half:BANK * half + BANK], seed_a[:, :], seed_b[:, BANK * half:BANK * half + BANK],
                                          start=True, stop=False, skip_group_check=True)
                        if u >= 2:
                            sums(g, u - 2)

                    r1 = r0 + (RING_S if g + 1 < NQ else 0)

                    def products(u):
                        pe.wait_ge(s["e2_done"], val(b, "e2_done", RING_R * g + 2 * (u + 1)))
                        todo = [(u, sc) for sc in columns(u) if not (u == 2 and sc[0][0] == 6)]
                        if u == 3:
                            todo.append((2, columns(2)[1]))
                        for uu, (strip, c) in todo:
                            for hh in range(QH):
                                mm = pe.matmul(st[32 * hh:32 * hh + 32, strip[1]:strip[2]], v1[:, strip[0], QH * g + hh, :],
                                               strip_e(uu, hh, c, strip),
                                               start=(strip[0] == 0), stop=False, skip_group_check=True)
                        if u == NU - 1:
                            mm.then_inc(s["pv_ready"], 1)

                    for u in range(NU + 1):
                        if u < NU:
                            for pair in range(2):
                                r = r1 + 2 * u + pair
                                pe.wait_ge(s["ring_free"], val(b, "ring_free", r - 1))
                                if u in (0, 2) and pair == 0:
                                    pe.wait_ge(s["rp_ready"], val(b, "rp_ready", 2 * g + (1 if u == 0 else 2)))
                                for i in range(2):
                                    hh = 2 * pair + i
                                    for (j, qa, qb), c in columns(u):
                                        mm = pe.matmul(ring[r % 2][:, BANK * i + c:BANK * i + c + qb - qa], sel[:, NB * hh + j, :], r_p[:, qa:qb],
                                                       start=True, stop=True, skip_group_check=True)
                                mm.then_inc(s["ring_ready"], 1)
                        if u == 0:
                            pe.wait_ge(s["e1_done"], val(b, "e1_done", QH * NU * (g + 1)))
                        if u >= 1:
                            products(u - 1)
                outputs(NQ - 1)

                pe.wait_ge(s["o_norm"], val(b, "o_norm", NQ))
                turn(USE_AT, None)
                for n in range(4):
                    ps = take(USE_O + n)
                    pe.wait_ge(s["dense_evac"], val(b, "dense_evac", USE_AT + (2 if n < 2 else 4)))
                    for i in range(2):
                        for k in range(NT):
                            mm = pe.matmul(ps[:, D * i:D * i + D], hT[:, k, P * (2 * n + i):P * (2 * n + i) + P], w_o[:, k, :],
                                           start=(k == 0), stop=(k == NT - 1))
                    mm.then_inc(s["dense_ready"], 1)
                turn(USE_HT2, 8)
                for half in range(2):
                    for f in range(NF):
                        ps = take(USE_F1 + NF * half + f)
                        if f == 0:
                            pe.wait_ge(s["dense_evac"], val(b, "dense_evac", USE_HT2 + 2 * half + 2))
                        for k in range(NT):
                            mm = pe.matmul(ps, w_fc[:, k, P * f:P * f + P], hT[:, k, BANK * half:BANK * half + BANK],
                                           start=(k == 0), stop=(k == NT - 1))
                        mm.then_inc(s["dense_ready"], 1)
                for n in range(4):
                    ps = take(USE_F2 + n)
                    pe.wait_ge(s["sq_done"], val(b, "sq_done", NF * (n // 2 + 1)))
                    for i in range(2):
                        for f in range(NF):
                            mm = pe.matmul(ps[:, D * i:D * i + D], gT[:, f, P * (2 * n + i):P * (2 * n + i) + P], w_proj[:, f, :],
                                           start=(f == 0), stop=(f == NF - 1))
                    mm.then_inc(s["dense_ready"], 1)

        @block.scalar
        def _(act):
            act.wait_ge(consts_in, 48)
            act.activation(c_e, c_T, ACT.Exp, scale=-1.0).then_inc(mod_step, 1)
            act.wait_ge(ready, 1)

            with act.Fori(0, B) as b:

                def rstd_guess(n):
                    act.wait_ge(s["ln_aggr"], val(b, "ln_aggr", n + 1))
                    act.activation(ln_a[:, :], mv[:, :, 1], ACT.Ln, bias=eps[:, 0:1]).then_inc(s["ln_log"], 1)
                    act.wait_ge(s["ln_log"], val(b, "ln_log", n + 1))
                    act.activation(rstd[:, :], ln_a[:, :], ACT.Exp, scale=-0.5).then_inc(s["ln_exp"], 1)

                def evac(use):
                    act.wait_ge(s["dense_ready"], val(b, "dense_ready", use + 1))
                    return bank(use)

                def modulate(use0, shift, scale):
                    for half in range(2):
                        for ft in range(NT):
                            ps = evac(use0 + NT * half + ft)
                            act.activation(hT[:, ft, BANK * half:BANK * half + BANK], ps, ACT.Identity,
                                           bias=modc[:, NT * shift + ft:NT * shift + ft + 1],
                                           scale=modc[:, NT * scale + ft:NT * scale + ft + 1]).then_inc(s["dense_evac"], 1)

                rstd_guess(0)
                act.wait_ge(s["mod_loaded"], val(b, "mod_loaded", 32))
                modulate(USE_HT1, 0, 1)
                for ot in range(NT):
                    for t in range(2):
                        for half in range(2):
                            ps = evac(USE_QK + 4 * ot + 2 * t + half)
                            act.activation(qk_f[:, 2 * ot + t, BANK * half:BANK * half + BANK], ps, ACT.Identity,
                                           bias=b_qk[:, t, ot:ot + 1]).then_inc(s["dense_evac"], 1)
                for n in range(4):
                    ps = evac(USE_V + n)
                    act.copy(v1[:, 2 * n:2 * n + 2, :, 0:DK],
                             ps.rearrange("p (i h d) -> p i h d", i=2, d=DK)).then_inc(s["dense_evac"], 1)
                ps = evac(USE_SUF)
                act.copy(suf[:, :, :], ps[:, 0:NQ * NB].rearrange("p (g i) -> p g i", g=NQ)).then_inc(s["dense_evac"], 1)
                act.wait_ge(s["stored0"], val(b, "stored0", 32))
                act.wait_ge(s["stored1"], val(b, "stored1", 32))
                act.wait_ge(s["xres_ready"], val(b, "xres_ready", 3))
                act.wait_ge(s["out_stored"], val(b, "out_stored", 16))

                def sum_log(g, half):
                    cols = slice(BANK * half, BANK * half + BANK)
                    n = 2 * g + half
                    act.wait_ge(s["d_ready"], val(b, "d_ready", n + 1))
                    act.activation(r_a[:, cols], dd[:, cols], ACT.Ln).then_inc(s["r_log"], 1)
                    act.wait_ge(s["r_log"], val(b, "r_log", n + 1))
                    act.activation(r_a[:, cols], r_a[:, cols], ACT.Exp, scale=-1.0).then_inc(s["r_exp"], 1)

                def sum_hi(g, half):
                    cols = slice(BANK * half, BANK * half + BANK)
                    act.wait_ge(s["r_newton"], val(b, "r_newton", 2 * (2 * g + half) + 2))
                    act.copy(r_h[:, cols], r_b[:, cols]).then_inc(s["r_hi"], 1)

                def sum_mid(g, half):
                    cols = slice(BANK * half, BANK * half + BANK)
                    act.wait_ge(s["r_rest"], val(b, "r_rest", 2 * g + half + 1))
                    act.copy(r_h[:, cols], r_a[:, cols]).then_inc(s["r_mid"], 1)

                for g in range(NQ):
                    for u in range(NU):
                        for hh in range(QH):
                            n = QH * (NU * g + u) + hh
                            act.wait_ge(s["st_ready"], val(b, "st_ready", n + 1))
                            act.activation(e[:, hh, BANK * u:BANK * u + BANK], st[:, BANK * (n % 2):BANK * (n % 2) + BANK],
                                           ACT.Exp, scale=DK ** -0.5).then_inc(s["e1_done"], 1)
                        if u == 5:
                            sum_log(g, 0)
                        if u == 6:
                            sum_hi(g, 0)
                        if u == 7:
                            sum_mid(g, 0)
                    sum_log(g, 1)
                    sum_hi(g, 1)
                    sum_mid(g, 1)
                    base = RING_S + g * (RING_S + RING_R) + (RING_S if g + 1 < NQ else 0)
                    for u in range(NU):
                        for pair in range(2):
                            act.wait_ge(s["ring_free"], val(b, "ring_free", base + 2 * u + pair + 1))
                            v = e[:, 2 * pair:2 * pair + 2, BANK * u:BANK * u + BANK]
                            act.activation(v, v, ACT.Exp).then_inc(s["e2_done"], 1)

                for half in range(2):
                    for ft in range(NT):
                        ps = evac(USE_AT + NT * half + ft)
                        act.copy(hT[:, ft, BANK * half:BANK * half + BANK], ps).then_inc(s["dense_evac"], 1)
                for n in range(4):
                    ps = evac(USE_O + n)
                    act.copy(tok[:, 2 * n:2 * n + 2, :], ps.rearrange("p (i d) -> p i d", i=2)).then_inc(s["dense_evac"], 1)
                rstd_guess(1)
                modulate(USE_HT2, 3, 4)
                for half in range(2):
                    for f in range(NF):
                        ps = evac(USE_F1 + NF * half + f)
                        act.activation(gT[:, f, BANK * half:BANK * half + BANK], ps, ACT.Relu).then_inc(s["dense_evac"], 1)
                for n in range(4):
                    ps = evac(USE_F2 + n)
                    act.activation(n1[:, BANK * n:BANK * n + BANK], ps, ACT.Copy, scale=-1.0).then_inc(s["dense_evac"], 1)

        @block.vector
        def _(dve):
            dve.wait_ge(mod_step, 1)
            dve.tensor_scalar(c_e, c_e, 1.0, None, ALU.add).then_inc(mod_step, 1)
            dve.wait_ge(mod_step, 2)
            dve.reciprocal(c_s, c_e).then_inc(mod_own, 1)
            dve.wait_ge(mod_own, 1)
            dve.tensor_tensor(c_s, c_s, c_T, ALU.mult).then_inc(mod_step, 1)
            dve.wait_ge(consts_in, 48)
            dve.tensor_copy(id_f[:, :], c_sb[:, C_ID:C_ID + P])
            dve.tensor_copy(id_b[:, :], c_sb[:, C_ID:C_ID + P])
            dve.tensor_copy(mask_q[:, :], c_sb[:, C_MQ:C_MQ + P])
            dve.tensor_copy(mask_t[:, :], c_sb[:, C_MT:C_MT + P])
            dve.tensor_copy(sel[:, :, :], c_sb[:, C_SEL:C_SEL + QH * NB].unsqueeze(2).to_broadcast([P, QH * NB, P]))
            dve.tensor_copy(d_ones[:, :, :], c_sb[:, C_DS:C_DS + 32 * NB].rearrange("p (j c) -> p j c", c=32))
            dve.tensor_copy(u_ind[:, :, :], c_sb[:, C_U:C_U + NB * NB].rearrange("p (j c) -> p j c", c=NB))
            dve.tensor_copy(seed_a[:, :], c_sb[:, C_SA:C_SA + P])
            dve.tensor_copy(seed_b[:, :], c_sb[:, C_OH:C_OH + S])
            dve.tensor_copy(ab[:, :], c_sb[:, C_AB:C_AB + 2])
            dve.memset(eps[:, :], EPS)
            dve.memset(q_st[KROWS:P, :, :, :], 0.0)
            dve.memset(negmax[:, :, :], 0.0)
            for par in range(2):
                for hh in range(QH):
                    dve.tensor_copy(k_st[KROWS:P, par, hh, :], c_sb[KROWS:P, C_OH:C_OH + S])
            dve.memset(v1[:, :, :, DK + 1:VW], 0.0)
            dve.memset(v1[:, :, :, DK:DK + 1], 1.0)
            dve.wait_ge(s_modmm, 1)
            for n in range(3):
                dve.tensor_copy(mod_sb[:, BANK * n:BANK * n + BANK], bank(n)[0:B, :]).then_inc(mod_own, 1)
            dve.wait_ge(mod_own, 4)
            g_v = mod_sb.rearrange("b (a c n) -> b a c n", a=2, c=3)
            gt = mod_t.rearrange("b (a n) -> b a n", a=2)
            ga = mod_u.rearrange("b (a n) -> b a n", a=2)
            dve.tensor_scalar(gt, g_v[:, :, 2, :], 0.0, 2.0, ALU.is_ge, ALU.mult).then_inc(mod_own, 1)
            dve.scalar_tensor_tensor(out=ga, in0=g_v[:, :, 2, :], scalar=-1.0, in1=g_v[:, :, 2, :],
                                     op0=ALU.mult, op1=ALU.max).then_inc(mod_own, 1)
            dve.tensor_scalar(g_v[:, :, 1, :], g_v[:, :, 1, :], 1.0, None, ALU.add).then_inc(mod_own, 1)
            dve.wait_ge(mod_own, 7)
            dve.tensor_scalar(ga, ga, 0.25, None, ALU.max).then_inc(mod_own, 1)
            dve.wait_ge(mod_own, 8)
            dve.scalar_tensor_tensor(out=g_v[:, :, 2, :], in0=gt, scalar=-1.0, in1=ga,
                                     op0=ALU.add, op1=ALU.mult).then_inc(mod_step, 6)
            dve.wait_ge(s["out_stored"], 16)
            dve.wait_ge(mod_step, 9)
            dve.engine_nop().then_inc(ready, 2)

            with dve.Fori(0, B) as b:
                def norm(n, src):
                    for i in range(NB):
                        if n:
                            dve.wait_ge(s["x2_ready"], val(b, "x2_ready", i // 2 + 1))
                        ins = dve.bn_stats(stats[:, i, :], src[:, i, :])
                    ins.then_inc(s["ln_stats"], 1)
                    dve.wait_ge(s["ln_stats"], val(b, "ln_stats", n + 1))
                    dve.memset(ln_b[:, :], 0.0)
                    for i in range(NB):
                        ins = dve.bn_aggr(mv[:, i, :], stats[:, i, :])
                    ins.then_inc(s["ln_aggr"], 1)
                    dve.wait_ge(s["ln_aggr"], val(b, "ln_aggr", n + 1))
                    dve.wait_ge(s["ln_exp"], val(b, "ln_exp", n + 1))
                    dve.scalar_tensor_tensor(out=ln_b[:, :], in0=mv[:, :, 1], scalar=EPS, in1=rstd[:, :],
                                             op0=ALU.add, op1=ALU.mult).then_inc(s["ln_newton"], 1)
                    dve.wait_ge(s["ln_newton"], val(b, "ln_newton", 4 * n + 1))
                    dve.tensor_tensor(ln_b[:, :], ln_b[:, :], rstd[:, :], ALU.mult).then_inc(s["ln_newton"], 1)
                    dve.wait_ge(s["ln_newton"], val(b, "ln_newton", 4 * n + 2))
                    dve.tensor_scalar(ln_b[:, :], ln_b[:, :], -0.5, 1.5, ALU.mult, ALU.add).then_inc(s["ln_newton"], 1)
                    dve.wait_ge(s["ln_newton"], val(b, "ln_newton", 4 * n + 3))
                    dve.tensor_tensor(rstd[:, :], ln_b[:, :], rstd[:, :], ALU.mult).then_inc(s["ln_newton"], 1)
                    dve.wait_ge(s["ln_newton"], val(b, "ln_newton", 4 * n + 4))
                    for i in range(NB):
                        dve.tensor_scalar(tok[:, i, :], src[:, i, :], mv[:, i, 0:1], rstd[:, i:i + 1],
                                          ALU.subtract, ALU.mult).then_inc(s["xn_ready"], 1)

                dve.wait_ge(s["x_loaded"], val(b, "x_loaded", 16))
                norm(0, x_in.rearrange("p (t d) -> p t d", t=NB))
                for n in range(4):
                    f = qk_f[:, n, :]
                    p3 = qk_p[:, n, :, :]
                    dve.wait_ge(s["dense_evac"], val(b, "dense_evac", USE_QK + 2 * n + 2))
                    dve.tensor_copy(p3[:, 0, :], f).then_inc(s["split"], 1)
                    dve.wait_ge(s["split"], val(b, "split", 4 * n + 1))
                    dve.tensor_tensor(f, f, p3[:, 0, :], ALU.subtract).then_inc(s["split"], 1)
                    dve.wait_ge(s["split"], val(b, "split", 4 * n + 2))
                    dve.tensor_copy(p3[:, 1, :], f).then_inc(s["split"], 1)
                    dve.wait_ge(s["split"], val(b, "split", 4 * n + 3))
                    dve.tensor_tensor(p3[:, 2, :], f, p3[:, 1, :], ALU.subtract).then_inc(s["split"], 1)

                def maxima(g, n, r):
                    kind, hh, t = RING[n]
                    head = QH * g + hh
                    slot = ring[r % 2]
                    dve.wait_ge(s["ring_ready"], val(b, "ring_ready", r + 1))
                    if kind == "s":
                        if t == 0 and head >= 2:
                            dve.wait_ge(s["max_lo"], val(b, "max_lo", head - 1))
                        w = min(8, 8 * NTILE) if t < NTILE - 1 else 4
                        dve.tensor_reduce(negmax[:, hh % 2, 8 * t:8 * t + w],
                                          slot[:, 0:P * w].rearrange("p (a n) -> p a n", n=P), AX_X, ALU.max,
                                          negate=True).then_inc(s["ring_free"], 1)
                        if t == NTILE - 1:
                            dve.wait_ge(s["ring_free"], val(b, "ring_free", r + 1))
                            dve.tensor_copy(maxp[:, hh % 2, :, 0], negmax[:, hh % 2, :]).then_inc(s["max_hi"], 1)
                            dve.wait_ge(s["max_hi"], val(b, "max_hi", head + 1))
                            dve.tensor_tensor(maxp[:, hh % 2, :, 1], negmax[:, hh % 2, :], maxp[:, hh % 2, :, 0],
                                              ALU.subtract).then_inc(s["max_lo"], 1)
                    else:
                        dve.tensor_copy(q_st[KROWS:KROWS + 16, g % 2, hh, :],
                                        slot[:, 0:BANK].bitcast(BF16)[KROWS:KROWS + 16, :]).then_inc(s["ring_free"], 1)

                def evac_products(g):
                    dve.wait_ge(s["pv_ready"], val(b, "pv_ready", g + 1))
                    dve.tensor_tensor(o_t[:, :].rearrange("p (i n) -> p i n", n=P), st[:, :].rearrange("p (i n) -> p i n", n=P),
                                      suf[:, g, :].unsqueeze(2).to_broadcast([P, NB, P]), ALU.add).then_inc(s["pv_evac"], 1)

                def divide_outputs(g):
                    dve.wait_ge(s["ot_ready"], val(b, "ot_ready", g + 1))
                    v = dd[:, :].rearrange("p (i h c) -> p i h c", i=NB, c=VW)
                    rc = o_rcp[:, :].rearrange("p (i h) -> p i h", h=QH)
                    dve.reciprocal(rc, v[:, :, :, DK]).then_inc(s["o_rec"], 1)
                    dve.wait_ge(s["o_rec"], val(b, "o_rec", g + 1))
                    dve.tensor_tensor(tok[:, :, QH * DK * g:QH * DK * (g + 1)].rearrange("p i (h d) -> p i h d", d=DK),
                                      v[:, :, :, 0:DK], rc.unsqueeze(3).to_broadcast([P, NB, QH, DK]),
                                      ALU.mult).then_inc(s["o_norm"], 1)

                def invert_a(g, half):
                    cols = slice(BANK * half, BANK * half + BANK)
                    n = 2 * g + half
                    dve.wait_ge(s["r_exp"], val(b, "r_exp", n + 1))
                    dve.tensor_tensor(r_b[:, cols], dd[:, cols], r_a[:, cols], ALU.mult).then_inc(s["r_newton"], 1)
                    dve.wait_ge(s["r_newton"], val(b, "r_newton", 2 * n + 1))
                    dve.scalar_tensor_tensor(out=r_b[:, cols], in0=r_b[:, cols], scalar=2.0, in1=r_a[:, cols],
                                             op0=ALU.subtract, op1=ALU.mult).then_inc(s["r_newton"], 1)

                def invert_b(g, half):
                    cols = slice(BANK * half, BANK * half + BANK)
                    n = 2 * g + half
                    dve.wait_ge(s["r_hi"], val(b, "r_hi", n + 1))
                    dve.scalar_tensor_tensor(out=r_a[:, cols], in0=r_h[:, cols], scalar=ab[:, 0:1], in1=r_b[:, cols],
                                             op0=ALU.mult, op1=ALU.add).then_inc(s["r_rest"], 1)

                def invert_c(g, half):
                    cols = slice(BANK * half, BANK * half + BANK)
                    n = 2 * g + half
                    dve.wait_ge(s["r_mid"], val(b, "r_mid", n + 1))
                    dve.scalar_tensor_tensor(out=r_p[:, cols], in0=r_h[:, cols], scalar=ab[:, 1:2], in1=r_a[:, cols],
                                             op0=ALU.mult, op1=ALU.add).then_inc(s["rp_ready"], 1)

                for n in range(RING_S):
                    maxima(0, n, n)
                for g in range(NQ):
                    r0 = RING_S + g * (RING_S + RING_R)
                    used = 0
                    for u in range(NU):
                        if g + 1 < NQ:
                            while used < RING_S * (u + 1) // NU:
                                maxima(g + 1, used, r0 + used)
                                used += 1
                        if u == 1 and g:
                            divide_outputs(g - 1)
                        if u == 6:
                            invert_a(g, 0)
                        if u == 7:
                            invert_b(g, 0)
                        if u == 8:
                            invert_c(g, 0)
                    invert_a(g, 1)
                    invert_b(g, 1)
                    invert_c(g, 1)
                    r1 = r0 + (RING_S if g + 1 < NQ else 0)
                    for u in range(NU):
                        for pair in range(2):
                            r = r1 + 2 * u + pair
                            dve.wait_ge(s["ring_ready"], val(b, "ring_ready", r + 1))
                            v = e[:, 2 * pair:2 * pair + 2, BANK * u:BANK * u + BANK]
                            dve.tensor_tensor(v, ring[r % 2][:, :].rearrange("p (i n) -> p i n", i=2), v,
                                              ALU.mult).then_inc(s["ring_free"], 1)
                    evac_products(g)
                divide_outputs(NQ - 1)

                for n in range(4):
                    t2 = tok[:, 2 * n:2 * n + 2, :]
                    dve.wait_ge(s["dense_evac"], val(b, "dense_evac", USE_O + n + 1))
                    dve.tensor_tensor(t2, t2, gates[:, 0:1, :].to_broadcast([P, 2, D]), ALU.mult).then_inc(s["ao"], 1)
                    dve.wait_ge(s["ao"], val(b, "ao", n + 1))
                    dve.tensor_tensor(x_res[:, 2 * n:2 * n + 2, :], x_res[:, 2 * n:2 * n + 2, :], t2, ALU.add).then_inc(s["x2_ready"], 1)
                norm(1, x_res)

                for n in range(4):
                    cols = slice(BANK * n, BANK * n + BANK)
                    dve.wait_ge(s["dense_evac"], val(b, "dense_evac", USE_F2 + n + 1))
                    dve.tensor_scalar(acc[:, cols], n1[:, cols], -1.0, None, ALU.is_lt).then_inc(s["lif"], 1)
                    mem, k = n1, 13 * n
                    for _ in range(4):
                        dve.scalar_tensor_tensor(out=lin[:, cols], in0=mem[:, cols], scalar=0.9, in1=n1[:, cols],
                                                 op0=ALU.mult, op1=ALU.add).then_inc(s["lif"], 1)
                        dve.wait_ge(s["lif"], val(b, "lif", k + 2))
                        dve.scalar_tensor_tensor(out=neg[:, cols], in0=mem[:, cols], scalar=-1.0, in1=lin[:, cols],
                                                 op0=ALU.is_lt, op1=ALU.add).then_inc(s["lif"], 1)
                        mem = neg
                        dve.wait_ge(s["lif"], val(b, "lif", k + 3))
                        dve.scalar_tensor_tensor(out=acc[:, cols], in0=mem[:, cols], scalar=-1.0, in1=acc[:, cols],
                                                 op0=ALU.is_lt, op1=ALU.add).then_inc(s["lif"], 1)
                        k += 3

        @block.gpsimd
        def _(pool):
            pool.wait_ge(ready, 1)
            pool.wait_ge(weights_in, 160)
            with pool.Fori(0, B) as b:
                pool.wait_ge(s["mod_loaded"], val(b, "mod_loaded", 32))
                pool.wait_ge(s["x_loaded"], val(b, "x_loaded", 16))
                pool.tensor_tensor(bo_g[:, :], b_o[:, :], gates[:, 0, :], ALU.mult).then_inc(s["xres_ready"], 1)
                pool.tensor_scalar(gb5[:, :], gates[:, 1, :], 0.2, None, ALU.mult).then_inc(s["xres_ready"], 1)
                pool.wait_ge(s["xres_ready"], val(b, "xres_ready", 2))
                pool.tensor_tensor(x_res[:, :, :], x_in.rearrange("p (t d) -> p t d", t=NB),
                                   bo_g[:, :].unsqueeze(1).to_broadcast([P, NB, D]), ALU.add).then_inc(s["xres_ready"], 1)
                pool.wait_ge(s["dense_evac"], val(b, "dense_evac", USE_V + 4))
                vv = v1[:, :, :, 0:DK]
                bb = b_v[:, :].rearrange("p (h d) -> p h d", d=DK)
                for i in range(NB):
                    ins = pool.tensor_tensor(vv[:, i, :, :], vv[:, i, :, :], bb, ALU.add)
                ins.then_inc(s["v_ready"], 1)
                for half in range(2):
                    for f in range(NF):
                        pool.wait_ge(s["dense_evac"], val(b, "dense_evac", USE_F1 + NF * half + f + 1))
                        v = gT[:, f, BANK * half:BANK * half + BANK]
                        pool.tensor_tensor(v, v, v, ALU.mult).then_inc(s["sq_done"], 1)
                for n in range(4):
                    a = acc[:, BANK * n:BANK * n + BANK].rearrange("p (i d) -> p i d", i=2)
                    pool.wait_ge(s["lif"], val(b, "lif", 13 * (n + 1)))
                    pool.tensor_tensor(a, a, gb5[:, :].unsqueeze(1).to_broadcast([P, 2, D]), ALU.mult).then_inc(s["fin"], 1)
                    pool.wait_ge(s["fin"], val(b, "fin", 2 * n + 1))
                    pool.tensor_tensor(a, a, x_res[:, 2 * n:2 * n + 2, :], ALU.add).then_inc(s["fin"], 1)


def kernel(**inputs):
    import numpy as _np
    import concourse.bacc as _bacc
    from concourse.bass_utils import run_bass_kernel_spmd as _run

    nc = _bacc.Bacc("TRN2", target_bir_lowering=False, num_devices=1)
    i = {k: _np.asarray(v) for k, v in inputs.items()}
    c = i["L0_c"]
    arrays = {
        "x": i["L0_attn_x"],
        "wqT": i["L0_attn_Wq_w"].T, "wkT": i["L0_attn_Wk_w"].T, "wvT": i["L0_attn_Wv_w"].T, "woT": i["L0_attn_Wo_w"].T,
        "bq": i["L0_attn_Wq_b"].reshape(NT, P).T, "bk": i["L0_attn_Wk_b"].reshape(NT, P).T, "bv": i["L0_attn_Wv_b"], "bo": i["L0_attn_Wo_b"],
        "wfcT": i["L0_ffn_W_fc"].T, "wprojT": i["L0_ffn_W_proj"].T,
        "cT": c.T.reshape(NT, P, B).transpose(1, 0, 2).reshape(P, NT * B),
        "wmod": i["L0_wmod"], "consts": constants(),
    }
    arrays = {f"in_{k}": _np.ascontiguousarray(v) for k, v in arrays.items()}
    args = [nc.dram_tensor(k, v.shape, F32, kind="ExternalInput").ap() for k, v in arrays.items()]
    out = nc.dram_tensor("out_0", (B, S, D), F32, kind="ExternalOutput").ap()
    build(nc, *args, out)
    r = _run(nc, [arrays], core_ids=[0])
    return r.results[0]["out_0"]
```

```python
from contextlib import ExitStack

import concourse.bass as bass
from concourse import mybir

F32 = mybir.dt.float32
BF16 = mybir.dt.bfloat16
ACT = mybir.ActivationFunctionType
ALU = mybir.AluOpType
AX_X = mybir.AxisListType.X

B, S, D, H, DK = 8, 1024, 256, 16, 16
FF = 4 * D
P = 128
NB = S // P
NT = D // P
NF = FF // P
QH = 4
NQ = H // QH
BANK = 512
EPS = 1e-5
MASKED = -1e30

QP = [0, 0, 0, 1, 1, 2]
KP = [0, 1, 2, 0, 1, 0]
KROWS = DK * len(QP)
VW = 32
ST_PARTS = 3

SPANS = [(0, 512), (512, 768), (768, 1024)]
UNITS = [
    [(0, 0, 512)],
    [(1, 128, 512), (3, 384, 512)],
    [(2, 256, 512), (0, 512, 768)],
    [(1, 512, 768), (2, 512, 768)],
    [(3, 512, 768), (4, 512, 768)],
    [(5, 640, 768), (7, 896, 1024), (0, 768, 1024)],
    [(1, 768, 1024), (2, 768, 1024)],
    [(3, 768, 1024), (4, 768, 1024)],
    [(5, 768, 1024), (6, 768, 1024)],
]
NU = len(UNITS)
SUMMED = {(2, 0): 0, (5, 0): 1, (NU - 1, 1): 2}
NEEDS = {0: 0, 2: 1, 5: 2}

TILES = [[(7, 0)], [(6, 0), (0, 896)], [(5, 0), (1, 768)], [(4, 0), (2, 640)], [(3, 0)]]
NTILE = len(TILES)
SLOTS = 8 * NTILE
SLOT_OF = {i: 8 * t + off // P for t, tile in enumerate(TILES) for i, off in tile}
RING_HEAD = NTILE + 1
RING_S = QH * RING_HEAD
RING_MAX = QH * NTILE
RING_R = NU * QH // 2


def columns(u):
    out, at = [], 0
    for strip in UNITS[u]:
        out.append((strip, at))
        at += strip[2] - strip[1]
    return out


def ring_order():
    out = []
    for hh in range(QH):
        for t in range(NTILE):
            out.append(("s", hh, t))
            if t == 1 and hh:
                out.append(("m", hh - 1, 0))
    return out + [("m", QH - 1, 0)]


RING = ring_order()

USE_HT1, USE_QK0, USE_V, USE_QK1, USE_SUM, USE_SUF = 0, 4, 8, 12, 16, 17
USES1 = 18
USE_AT, USE_O, USE_HT2, USE_F1, USE_F2 = 0, 4, 8, (12, 22), (20, 30)
USES2 = 32

SPREAD = [(12, 35), (-1, 35), (-1, 35), (-1, 35)]
EARLY_AT = {4: 1, 5: 1, 6: 2, 7: 1, NF: 3}
EARLY = sum(EARLY_AT.values())
BETWEEN = [{1: USE_HT1, 3: USE_HT1 + 1, 5: USE_HT1 + 2, 7: USE_HT1 + 3},
           {0: USE_QK0, 2: USE_QK0 + 1, 6: USE_QK0 + 2, 8: USE_QK0 + 3}]

SUMS_AT = {(2, 2): [(0, 0)], (2, 3): [(0, 1)], (3, 0): [(1, 0)], (3, 1): [(1, 1)], (3, 2): [(2, 0)], (3, 3): [(2, 1)]}
for _u in range(4, NU):
    SUMS_AT[_u, 1] = [(_u - 1, 0)]
    SUMS_AT[(_u, 3) if _u != 6 else (7, 0)] = [(_u - 1, 1)]

SUM_STEPS = {(4, 0): [("log", 0)], (4, 2): [("exp", 0)], (5, 1): [("hi", 0)], (6, 1): [("mid", 0)], (6, 2): [("copy", 1)],
             (7, 0): [("log", 1)], (7, 1): [("exp", 1)], (8, 0): [("hi", 1)], (8, 2): [("mid", 1)]}
INVERT = {4: 0, 7: 1}

PER = {
    "xin_loaded": 16, "mod1_loaded": 16, "xres_loaded": 16, "mod2_loaded": 32, "ffn_loaded": 48,
    "ln1_stats": 1, "ln1_aggr": 1, "ln1_log": 1, "ln1_exp": 1, "ln1_newton": 4, "xn1_ready": NB,
    "ln2_stats": 1, "ln2_aggr": 1, "ln2_log": 1, "ln2_exp": 1, "ln2_newton": 4, "xn2_ready": NB,
    "d1_ready": USES1, "d1_evac": USES1, "d2_ready": USES2, "d2_evac": USES2, "split0": 6, "split1": 6,
    "stored0": 32, "stored1": 32, "stack0": 384, "stack1": 384, "ring_ready": NQ * (RING_S + RING_R),
    "ring_free": NQ * (RING_MAX + RING_R), "turned": H, "max_hi": H, "max_lo": H, "st_ready": NQ * NU * QH,
    "e1_done": NQ * NU * QH, "d_ready": len(SPANS) * NQ, "d_copied": NQ, "r_log": len(SPANS) * NQ,
    "r_exp": len(SPANS) * NQ, "r_newton": 2 * len(SPANS) * NQ,
    "r_hi": len(SPANS) * NQ, "r_rest": len(SPANS) * NQ, "r_mid": len(SPANS) * NQ, "rp_ready": len(SPANS) * NQ, "e2_done": NQ * RING_R,
    "pv_ready": NQ, "pv_evac": 2 * NQ, "ot_ready": NQ, "o_rec": NQ, "o_norm": NQ, "v_ready": 1,
    "xres_ready": 3, "ao": 4, "x2_ready": 4, "sq_done": 16, "lif": 52, "fin": 8, "out_stored": 64,
}

C_ID, C_MQ, C_MT, C_SEL, C_DS, C_U, C_SA, C_OH, C_AB = 0, 128, 256, 384, 416, 672, 736, 864, 1888
C_END = 1890


def constants():
    import numpy as np

    c = np.zeros((P, C_END), np.float32)
    r = np.arange(P)
    c[:, C_ID:C_ID + P] = np.eye(P)
    c[:, C_MQ:C_MQ + P] = MASKED * (r[None, :] > r[:, None])
    c[:, C_MT:C_MT + P] = MASKED * (r[:, None] > r[None, :])
    for hh in range(QH):
        for j in range(NB):
            for part in range(ST_PARTS):
                c[32 * hh + 8 * part + j, C_SEL + NB * hh + j] = -1.0
    for j in range(NB):
        for part in range(ST_PARTS):
            c[:, C_DS + 32 * j + 8 * part + j] = 1.0
        c[:, C_U + NB * j:C_U + NB * j + j] = 1.0
    for i in range(NB):
        c[i, C_SA:C_SA + P] = (r % 32 >= 8 * ST_PARTS) | (r % 8 > i)
        for row in (i, KROWS + 2 * i, KROWS + 2 * i + 1):
            c[row, C_OH + P * i:C_OH + P * (i + 1)] = 1.0
    c[:, C_AB] = -1.0 * (r % 32 >= 8)
    c[:, C_AB + 1] = -1.0 * (r % 32 >= 16)
    return c


def build(nc, x, wqT, wkT, wvT, woT, bq, bk, bv, bo, wfcT, wprojT, cT, wmod, consts, out):
    mod_dram = nc.dram_tensor("mod_scratch", (B, 6 * D), F32).ap()
    part_dram = [nc.dram_tensor(f"{n}_parts", (3, D, S), BF16).ap() for n in "qk"]

    with ExitStack() as ctx:
        def sb(name, shape, dt=F32):
            return ctx.enter_context(nc.sbuf_tensor(name, shape, dt))

        def sem(name):
            return ctx.enter_context(nc.semaphore(name))

        x_res = sb("x_res", [P, NB, D])
        x_in = sb("x_in", [P, NB, D])
        tok = sb("tok", [P, NB, D])
        hT1 = sb("hT1", [P, NT, S])
        hT2 = sb("hT2", [P, NT, S])
        q_st = sb("q_st", [P, 2, QH, S], BF16)
        k_st = sb("k_st", [P, 2, QH, S], BF16)
        v1 = sb("v1", [P, NB, H, VW])
        e = sb("e", [P, QH, NU * BANK])
        ef = e[:, :, :].rearrange("p h n -> p (h n)")
        w_fc = e[:, 0:NT, 4 * BANK:6 * BANK]
        w_proj = e[:, NT:QH, 4 * BANK:6 * BANK].rearrange("p h (f n) -> p h f n", n=D)
        n1 = e[:, :, 7 * BANK:8 * BANK]
        acc = e[:, :, 8 * BANK:9 * BANK]

        def gT(f):
            return e[:, f // 2, S * (f % 2):S * (f % 2) + S]

        qk_f = sb("qk_f", [P, S])
        qk_p = sb("qk_p", [P, 2, 3, S], BF16)
        w_q, w_k, w_v, w_o = (sb(n, [P, NT, D]) for n in ("w_q", "w_k", "w_v", "w_o"))
        b_qk = sb("b_qk", [P, 2, NT])
        b_v = sb("b_v", [P, D])
        b_o = sb("b_o", [P, D])
        modc1 = sb("modc1", [P, 3 * NT])
        modc2 = sb("modc2", [P, 3 * NT])
        gates = sb("gates", [P, 2, D])
        bo_g = sb("bo_g", [P, D])
        r_a = sb("r_a", [P, S])
        r_b = sb("r_b", [P, S])
        r_h = sb("r_h", [P, S], BF16)
        r_p = sb("r_p", [P, S], BF16)
        o_t = r_a
        neg, lin = r_a, r_b
        suf = sb("suf", [P, NQ, NB])
        o_rcp = sb("o_rcp", [P, NB * QH])
        negmax = sb("negmax", [P, 2, SLOTS])
        maxp = sb("maxp", [P, 2, SLOTS, 2], BF16)
        stats = sb("stats", [P, NB, 6])
        mv = sb("mv", [P, NB, 2])
        rstd = sb("rstd", [P, NB])
        ln_a = sb("ln_a", [P, NB])
        ln_b = sb("ln_b", [P, NB])
        eps = sb("eps", [P, 1])
        ab = sb("ab", [P, 2])
        id_f = sb("id_f", [P, P])
        id_b = sb("id_b", [P, P], BF16)
        mask_q = sb("mask_q", [P, P], BF16)
        mask_t = sb("mask_t", [P, P], BF16)
        sel = sb("sel", [P, QH * NB], BF16)
        d_ones = sb("d_ones", [P, NB, 32])
        u_ind = sb("u_ind", [P, NB, NB])
        seed_a = sb("seed_a", [P, P], BF16)
        seed_b = sb("seed_b", [P, S], BF16)
        suf_t = tok[:, 0:2, :].rearrange("i a n -> i (a n)").rearrange("i (h c) -> i h c", h=H)
        c_sb = ef[:, 0:C_END]
        wmod_sb = ef[:, 4 * S:4 * S + NT * 6 * D].rearrange("p (k n) -> p k n", k=NT)
        c_T = ef[:, 8 * S:8 * S + NT * B]
        c_e = ef[:, 9 * S:9 * S + NT * B]
        c_s = ef[:, 10 * S:10 * S + NT * B]
        mod_sb = ef[0:B, 12 * S:12 * S + 6 * D]
        mod_t = ef[0:B, 14 * S:14 * S + 2 * D]
        mod_u = ef[0:B, 14 * S + 2 * D:14 * S + 4 * D]

        ring = [ctx.enter_context(nc.psum_tensor(f"ring{i}", [P, 2 * BANK], F32)) for i in range(2)]
        st = ctx.enter_context(nc.psum_tensor("st", [P, 2 * BANK], F32))
        dd = ctx.enter_context(nc.psum_tensor("dd", [P, 2 * BANK], F32))

        def bank1(i):
            if i < USE_V:
                return dd[:, 0:BANK]
            return ring[i % 4 // 2][:, BANK * (i % 2):BANK * (i % 2) + BANK]

        def bank2(i):
            return [st, dd][i % 4 // 2][:, BANK * (i % 2):BANK * (i % 2) + BANK]

        s = {n: sem(n) for n in PER}
        weights_in, consts_in, ready, mod_step = (
            sem(n) for n in ("weights_in", "consts_in", "ready", "mod_step"))
        s_modmm = sem("mod_product")
        mod_own = sem("mod_own")

        def val(b, name, n):
            return b * PER[name] + n

        def strip_e(u, hh, c, strip):
            at = BANK * u + c
            return e[:, hh, at:at + strip[2] - strip[1]]

        def ring_base(g, last):
            at = g * (RING_S + RING_R)
            return at, at + (0 if last and g == NQ - 1 else RING_S)

        def s_target(g, n):
            start, end = SPREAD[g]
            done = 0 if g else EARLY
            return min(RING_S - 1, done + max(0, (RING_S - 1 - done) * (n + 1 - start) // (end - start)))

        def freed(r, last):
            g, n = divmod(r, RING_S + RING_R)
            if last and g == NQ - 1:
                return "ring_free", (RING_MAX + RING_R) * g + n + 1
            if n < RING_S and RING[n][0] == "m":
                return "turned", QH * g + RING[n][1] + 1
            read = sum(use[0] == "s" for use in RING[:n + 1]) + max(0, n + 1 - RING_S)
            return "ring_free", (RING_MAX + RING_R) * g + read

        first = {"ring_ready": RING_S, "ring_free": RING_MAX, "turned": QH}

        def wait_ring(eng, b, name, n):
            eng.wait_ge(s[name], first[name] + val(b, name, n))

        def rows(eng, row):
            with eng.Fori(0, B - 1) as b:
                row(b, False)
            row(B - 1, True)

        block = ctx.enter_context(nc.Block())

        @block.sync
        def _(sp):
            sp.dma_start(c_sb, consts).then_inc(consts_in, 16)
            sp.dma_start(c_T, cT).then_inc(consts_in, 16)
            sp.dma_start(wmod_sb, wmod.rearrange("(k p) n -> p k n", p=P)).then_inc(consts_in, 16)
            x_rows = x.rearrange("b (t p) d -> p b t d", p=P)

            def load_x(r):
                sp.dma_start(x_in[:, :, :].rearrange("p (b t) d -> p b t d", b=1), x_rows[:, bass.ds(r, 1), :, :]).then_inc(s["xin_loaded"], 16)

            load_x(0)
            for t, w in ((w_q, wqT), (w_k, wkT), (w_v, wvT), (w_o, woT)):
                sp.dma_start(t[:, :, :], w.rearrange("(k p) n -> p k n", p=P)).then_inc(weights_in, 16)
            for n, v in enumerate((bq, bk)):
                sp.dma_start(b_qk[:, n, :], v).then_inc(weights_in, 16)
            for t, v in ((b_v, bv), (b_o, bo)):
                sp.dma_start(t[:, :], v.rearrange("(a n) -> a n", a=1).to_broadcast([P, D])).then_inc(weights_in, 16)
            sp.wait_ge(mod_step, 9)
            sp.dma_start(mod_dram, mod_sb).then_inc(s["out_stored"], 16)
            sp.wait_ge(s["out_stored"], 16)
            o_rows = out.rearrange("b (t p) d -> p b t d", p=P)
            mod_cols = mod_dram.rearrange("b (m n p) -> p b m n", p=P, n=3 * NT)
            mod_rows = mod_dram.rearrange("b (a c n) -> b a c n", a=2, c=3)

            def load_mod1(r):
                sp.dma_start(modc1[:, :].rearrange("p (b n) -> p b n", b=1), mod_cols[:, bass.ds(r, 1), 0, :],
                             allow_slow_non_contiguous=True).then_inc(s["mod1_loaded"], 16)

            def store_parts(r, ot):
                for t in range(2):
                    sp.wait_ge(s[f"split{ot}"], val(r, f"split{ot}", 3 * t + 3))
                    sp.dma_start(part_dram[t][:, P * ot:P * ot + P, :].rearrange("a p n -> p a n"),
                                 qk_p[:, t, :, :]).then_inc(s[f"stored{ot}"], 16)

            def load_stacks(r, g):
                f0 = QH * DK * g
                for stack, parts, dram in ((q_st, QP, part_dram[0]), (k_st, KP, part_dram[1])):
                    for n, a in enumerate(parts):
                        sp.dma_start(stack[DK * n:DK * n + DK, g % 2, :, :],
                                     dram[a, f0:f0 + QH * DK, :].rearrange("(h d) n -> d h n", h=QH),
                                     ).then_inc(s[f"stack{g % 2}"], 16)

            load_mod1(0)
            sp.wait_ge(ready, 1)
            store_parts(0, 0)
            load_x(1)
            sp.wait_ge(s["stored0"], 32)
            load_stacks(0, 0)
            load_stacks(0, 1)
            store_parts(0, 1)

            def row(b, last):
                def scored(g):
                    sp.wait_ge(s["st_ready"], val(b, "st_ready", NU * QH * (g + 1)))

                if not last:
                    b_next = sp.snap(b + 1)
                    b_after = sp.snap((b + 2) % B)
                sp.dma_start(x_res[:, :, :].rearrange("p (b t) d -> p b t d", b=1), x_rows[:, bass.ds(b, 1), :, :]).then_inc(s["xres_loaded"], 16)
                sp.dma_start(modc2[:, :].rearrange("p (b n) -> p b n", b=1), mod_cols[:, bass.ds(b, 1), 1, :],
                             allow_slow_non_contiguous=True).then_inc(s["mod2_loaded"], 16)
                sp.dma_start(gates[:, :, :], mod_rows[bass.ds(b, 1), :, 2, :].to_broadcast([P, 2, D])).then_inc(s["mod2_loaded"], 16)
                if not last:
                    load_mod1(b_next)
                stored = val(b, "stored1", 32) if last else sp.snap(val(b, "stored1", 32))
                scored(0)
                sp.wait_ge(s["stored1"], stored)
                load_stacks(b, 2)
                scored(1)
                load_stacks(b, 3)
                if not last:
                    store_parts(b + 1, 0)
                    load_x(b_after)
                    stored = sp.snap(val(b + 1, "stored0", 32))
                    scored(2)
                    sp.wait_ge(s["stored0"], stored)
                    load_stacks(b + 1, 0)
                    scored(3)
                    load_stacks(b + 1, 1)
                sp.wait_ge(s["pv_ready"], val(b, "pv_ready", NQ))
                sp.dma_start(w_fc, wfcT.rearrange("(k p) n -> p k n", p=P)).then_inc(s["ffn_loaded"], 16)
                for h in range(2):
                    sp.dma_start(w_proj[:, h, :, :], wprojT.rearrange("(h f p) n -> h p f n", p=P, h=2)[h]).then_inc(s["ffn_loaded"], 16)
                if not last:
                    store_parts(b + 1, 1)
                for c in range(4):
                    sp.wait_ge(s["fin"], val(b, "fin", 2 * c + 2))
                    sp.dma_start(o_rows[:, bass.ds(b, 1), 2 * c:2 * c + 2, :],
                                 acc[:, c, :].rearrange("p (b t d) -> p b t d", b=1, t=2),
                                 ).then_inc(s["out_stored"], 16)

            rows(sp, row)
            sp.wait_ge(s["out_stored"], 16 + B * PER["out_stored"])

        @block.tensor
        def _(pe):
            pe.wait_ge(consts_in, 48)
            pe.wait_ge(mod_step, 3)
            for n in range(3):
                for k in range(NT):
                    mm = pe.matmul(bank1(USE_V + n)[0:B, :], c_s[:, B * k:B * k + B], wmod_sb[:, k, BANK * n:BANK * n + BANK],
                                   start=(k == 0), stop=(k == NT - 1))
            mm.then_inc(s_modmm, 1)
            pe.wait_ge(weights_in, 128)
            pe.wait_ge(ready, 2)

            def take1(r, use):
                back = 1 if use < USE_V else 4
                if use >= back and not USE_V <= use < USE_V + 4:
                    pe.wait_ge(s["d1_evac"], val(r, "d1_evac", use - back + 1))
                return bank1(use)

            def take2(b, use):
                if use >= 4:
                    pe.wait_ge(s["d2_evac"], val(b, "d2_evac", use - 3))
                return bank2(use)

            def turn(take, r, use0, n, done, src, normed):
                half, ft = n // NT, n % NT
                ps = take(r, use0 + n)
                if normed:
                    pe.wait_ge(s[normed], val(r, normed, 4 * half + 4))
                for i in range(4):
                    mm = pe.transpose(ps[:, P * i:P * i + P], src[:, 4 * half + i, P * ft:P * ft + P], id_f[:, :])
                mm.then_inc(s[done], 1)

            def project_qk(r, ot, n):
                t, half = n // 2, n % 2
                ps = take1(r, (USE_QK0, USE_QK1)[ot] + n)
                for k in range(NT):
                    mm = pe.matmul(ps, (w_q, w_k)[t][:, k, P * ot:P * ot + P], hT1[:, k, BANK * half:BANK * half + BANK],
                                   start=(k == 0), stop=(k == NT - 1))
                mm.then_inc(s["d1_ready"], 1)

            def tokens_by(ps, src, n, w):
                for i in range(2):
                    for k in range(NT):
                        mm = pe.matmul(ps[:, D * i:D * i + D], src[:, k, P * (2 * n + i):P * (2 * n + i) + P], w[:, k, :],
                                       start=(k == 0), stop=(k == NT - 1))
                return mm

            def project_v(r, n):
                tokens_by(take1(r, USE_V + n), hT1, n, w_v).then_inc(s["d1_ready"], 1)

            def behind(r):
                ps = take1(r, USE_SUM)
                pe.wait_ge(s["v_ready"], val(r, "v_ready", 1))
                for j in range(1, NB):
                    mm = pe.matmul(ps[0:NB, 0:H * (DK + 1)], u_ind[:, j, :], v1[:, j, :, 0:DK + 1],
                                   start=(j == 1), stop=(j == NB - 1))
                mm.then_inc(s["d1_ready"], 1)

            def behind_turned(r):
                pe.wait_ge(s["d1_evac"], val(r, "d1_evac", USE_SUM + 1))
                ps = bank1(USE_SUF)
                for g in range(NQ):
                    mm = pe.transpose(ps[:, P * g:P * g + P], suf_t[:, QH * g:QH * g + QH, :].rearrange("i h c -> i (h c)"), id_f[:, :])
                mm.then_inc(s["d1_ready"], 1)

            def ring_use(b, g, n, r, prologue=False):
                kind, hh, t = RING[n]
                par = g % 2
                slot = ring[r % 2]
                if r >= 2:
                    name, k = freed(r - 2, False)
                    if prologue:
                        pe.wait_ge(s[name], k)
                    else:
                        wait_ring(pe, b, name, k)
                if n == 0:
                    pe.wait_ge(s[f"stack{par}"], val(b, f"stack{par}", 192 * (g // 2 + 1)))
                if kind == "s":
                    for i, off in TILES[t]:
                        q = q_st[0:KROWS, par, hh, P * i:P * i + P]
                        c, end, diag = off, off + P * (i + 1), off + P * i
                        while c < end:
                            stop = min(end, (c // BANK + 1) * BANK)
                            last = c <= diag < stop
                            mm = pe.matmul(slot[:, c:stop], q, k_st[0:KROWS, par, hh, c - off:stop - off],
                                           start=True, stop=not last, skip_group_check=True)
                            if last:
                                mm = pe.matmul(slot[:, diag:diag + P], id_b[:, :], mask_q[:, :],
                                               start=False, stop=True, skip_group_check=True)
                            c = stop
                else:
                    pe.wait_ge(s["max_lo"], val(b, "max_lo", QH * g + hh + 1))
                    view = slot[:, 0:BANK].bitcast(BF16)
                    for i in range(NB):
                        at = SLOT_OF[i]
                        mm = pe.transpose(view[KROWS:KROWS + 16, P * i:P * i + P], maxp[:, hh % 2, at:at + NB, :].rearrange("p w a -> p (w a)"), id_b[:, :])
                mm.then_inc(s["ring_ready"], 1)

            for n in range(4):
                turn(take1, 0, USE_HT1, n, "d1_ready", x_in, "xn1_ready")
            for n in range(4):
                project_qk(0, 0, n)
            for n in range(4):
                project_v(0, n)
            for n in range(4):
                project_qk(0, 1, n)
            behind(0)
            behind_turned(0)
            pe.wait_ge(s["d1_evac"], USES1)
            for n in range(RING_S):
                ring_use(0, 0, n, n, True)
            pe.wait_ge(s["ring_free"], RING_MAX)
            pe.wait_ge(s["turned"], QH)
            for n in range(EARLY):
                ring_use(0, 1, n, n)

            def row(b, last):
                def sums(g, u, part):
                    pe.wait_ge(s["e1_done"], val(b, "e1_done", QH * (NU * g + u + 1)))
                    pieces = columns(u)
                    if len(pieces) == 1:
                        (j, qa, qb), _ = pieces[0]
                        mid = (qb - qa) // 2
                        pieces = [((j, qa, qa + mid), 0), ((j, qa + mid, qb), mid)]
                    if (u, part) == (5, 1):
                        pe.wait_ge(s["d_copied"], val(b, "d_copied", g + 1))
                    for strip, c in pieces[1:] if part else pieces[:1]:
                        for hh in range(QH):
                            mm = pe.matmul(dd[32 * hh:32 * hh + 32, strip[1]:strip[2]], d_ones[:, strip[0], :], strip_e(u, hh, c, strip),
                                           start=False, stop=False, skip_group_check=True)
                    if (u, part) in SUMMED:
                        mm.then_inc(s["d_ready"], 1)

                def one_over_sums(g, r1, u, pairs=(0, 1)):
                    for pair in pairs:
                        r = r1 + 2 * u + pair
                        wait_ring(pe, b, *freed(r - 2, last))
                        if u in NEEDS and pair == 0:
                            pe.wait_ge(s["rp_ready"], val(b, "rp_ready", len(SPANS) * g + NEEDS[u] + 1))
                        for i in range(2):
                            hh = 2 * pair + i
                            for (j, qa, qb), c in columns(u):
                                mm = pe.matmul(ring[r % 2][:, BANK * i + c:BANK * i + c + qb - qa], sel[:, NB * hh + j:NB * hh + j + 1].to_broadcast([P, P]), r_p[:, qa:qb],
                                               start=True, stop=True, skip_group_check=True)
                        mm.then_inc(s["ring_ready"], 1)

                def outputs(g):
                    if g < len(BETWEEN) and not last:
                        pe.wait_ge(s["d1_evac"], val(b + 1, "d1_evac", 4 * g + 4))
                    for i in range(NB):
                        if i % 4 == 0:
                            pe.wait_ge(s["pv_evac"], val(b, "pv_evac", 2 * g + i // 4 + 1))
                        mm = pe.transpose(dd[:, P * i:P * i + P], o_t[:, P * i:P * i + P], id_f[:, :])
                    mm.then_inc(s["ot_ready"], 1)

                for g in range(NQ):
                    r0, r1 = ring_base(g, last)
                    used = 0 if g else EARLY
                    for u in range(NU):
                        for hh in range(QH):
                            if r1 > r0:
                                while used < s_target(g, QH * u + hh):
                                    ring_use(b, g + 1, used, r0 + used)
                                    used += 1
                            n = QH * (NU * g + u) + hh
                            slot = st[:, BANK * (n % 2):BANK * (n % 2) + BANK]
                            if n % (NU * QH) < 2:
                                if g:
                                    pe.wait_ge(s["pv_evac"], val(b, "pv_evac", 2 * g - 1 + n % 2))
                            else:
                                pe.wait_ge(s["e1_done"], val(b, "e1_done", n - 1))
                            if u == 0 and g:
                                wait_ring(pe, b, "turned", QH * (g - 1) + hh + 1)
                            for (j, qa, qb), c in columns(u):
                                diag = qa == P * j
                                mm = pe.matmul(slot[:, c:c + qb - qa], k_st[:, g % 2, hh, P * j:P * j + P], q_st[:, g % 2, hh, qa:qb],
                                               start=True, stop=not diag, skip_group_check=True)
                                if diag:
                                    mm = pe.matmul(slot[:, c:c + P], id_b[:, :], mask_t[:, :],
                                                   start=False, stop=True, skip_group_check=True)
                            mm.then_inc(s["st_ready"], 1)
                            if u == 1 and hh == QH - 1 and g:
                                outputs(g - 1)
                            if u == 2 and hh == 1:
                                if g:
                                    pe.wait_ge(s["o_norm"], val(b, "o_norm", g))
                                for half in range(2):
                                    pe.matmul(dd[:, BANK * half:BANK * half + BANK], seed_a[:, :], seed_b[:, BANK * half:BANK * half + BANK],
                                              start=True, stop=False, skip_group_check=True)
                            for uu, part in SUMS_AT.get((u, hh), ()):
                                sums(g, uu, part)
                    if r1 > r0:
                        ring_use(b, g + 1, RING_S - 1, r1 - 1)
                    one_over_sums(g, r1, 0, (0,))
                    sums(g, NU - 1, 0)
                    one_over_sums(g, r1, 0, (1,))
                    sums(g, NU - 1, 1)

                    def products(u):
                        pe.wait_ge(s["e2_done"], val(b, "e2_done", RING_R * g + 2 * (u + 1)))
                        if u == 0:
                            pe.matmul(st[:, BANK:2 * BANK], id_b[:, :], mask_t[:, P - 1:P].to_broadcast([P, BANK]),
                                      start=True, stop=False, skip_group_check=True)
                        for strip, c in columns(u):
                            for hh in range(QH):
                                mm = pe.matmul(st[32 * hh:32 * hh + 32, strip[1]:strip[2]], v1[:, strip[0], QH * g + hh, :],
                                               strip_e(u, hh, c, strip), start=(u == 0), stop=False, skip_group_check=True)
                        if u == NU - 1:
                            mm.then_inc(s["pv_ready"], 1)

                    for u in range(NU + 2):
                        if 0 < u < NU:
                            one_over_sums(g, r1, u)
                        if u == 1:
                            pe.wait_ge(s["e1_done"], val(b, "e1_done", QH * NU * (g + 1)))
                        if g < len(BETWEEN) and not last and u in BETWEEN[g]:
                            use = BETWEEN[g][u]
                            if use < USE_QK0:
                                turn(take1, b + 1, USE_HT1, use - USE_HT1, "d1_ready", x_in, "xn1_ready")
                            else:
                                project_qk(b + 1, 0, use - USE_QK0)
                        if u == 1:
                            products(0)
                        if u >= 3:
                            products(u - 2)
                if not last:
                    wait_ring(pe, b, "ring_free", PER["ring_free"])
                    project_v(b + 1, 0)
                outputs(NQ - 1)
                if not last:
                    project_v(b + 1, 1)
                pe.wait_ge(s["o_norm"], val(b, "o_norm", NQ))
                for n in range(4):
                    turn(take2, b, USE_AT, n, "d2_ready", tok, None)
                if not last:
                    project_v(b + 1, 2)
                for n in range(4):
                    ps = take2(b, USE_O + n)
                    pe.wait_ge(s["d2_evac"], val(b, "d2_evac", USE_AT + (2 if n < 2 else 4)))
                    tokens_by(ps, hT2, n, w_o).then_inc(s["d2_ready"], 1)
                if not last:
                    project_v(b + 1, 3)
                    for n in range(4):
                        project_qk(b + 1, 1, n)
                for n in range(4):
                    turn(take2, b, USE_HT2, n, "d2_ready", tok, "xn2_ready")
                pe.wait_ge(s["ffn_loaded"], val(b, "ffn_loaded", 48))
                early = 0
                for half in range(2):
                    for f in range(NF):
                        ps = take2(b, USE_F1[half] + f)
                        if f == 0:
                            pe.wait_ge(s["d2_evac"], val(b, "d2_evac", USE_HT2 + 2 * half + 2))
                        for k in range(NT):
                            mm = pe.matmul(ps, w_fc[:, k, P * f:P * f + P], hT2[:, k, BANK * half:BANK * half + BANK],
                                           start=(k == 0), stop=(k == NT - 1))
                        mm.then_inc(s["d2_ready"], 1)
                        if half and not last and f in EARLY_AT:
                            if early == 0:
                                pe.wait_ge(s["d1_evac"], val(b + 1, "d1_evac", USES1))
                            for _ in range(EARLY_AT[f]):
                                ring_use(b + 1, 1, early, early)
                                early += 1
                    if not half and not last:
                        behind(b + 1)
                    for n in range(2 * half, 2 * half + 2):
                        ps = take2(b, USE_F2[half] + n % 2)
                        for i in range(2):
                            for f in range(NF):
                                if n == 2 * half and i == 0:
                                    pe.wait_ge(s["sq_done"], val(b, "sq_done", NF * half + f + 1))
                                mm = pe.matmul(ps[:, D * i:D * i + D], gT(f)[:, P * (2 * n + i):P * (2 * n + i) + P],
                                               w_proj[:, f // 4, f % 4, :], start=(f == 0), stop=(f == NF - 1))
                            if (n, i) == (2, 0) and not last:
                                for _ in range(EARLY_AT.get(NF, 0)):
                                    ring_use(b + 1, 1, early, early)
                                    early += 1
                        mm.then_inc(s["d2_ready"], 1)
                        if n == 0 and not last:
                            behind_turned(b + 1)
                if not last:
                    pe.wait_ge(s["d2_evac"], val(b, "d2_evac", USES2))

            rows(pe, row)

        @block.scalar
        def _(act):
            act.preload_act_table_set("natural_log_exp_and_others")
            act.wait_ge(consts_in, 48)
            act.activation(c_e, c_T, ACT.Exp, scale=-1.0).then_inc(mod_step, 1)

            def rstd_guess(r, ln):
                act.wait_ge(s[ln + "_aggr"], val(r, ln + "_aggr", 1))
                act.activation(ln_a[:, :], mv[:, :, 1], ACT.Ln, bias=eps[:, 0:1]).then_inc(s[ln + "_log"], 1)
                act.wait_ge(s[ln + "_log"], val(r, ln + "_log", 1))
                act.activation(rstd[:, :], ln_a[:, :], ACT.Exp, scale=-0.5).then_inc(s[ln + "_exp"], 1)

            def evac1(r, use):
                act.wait_ge(s["d1_ready"], val(r, "d1_ready", use + 1))
                return bank1(use)

            def evac2(b, use):
                act.wait_ge(s["d2_ready"], val(b, "d2_ready", use + 1))
                return bank2(use)

            def modulate(evac, r, use0, n, hT, modc, done):
                half, ft = n // NT, n % NT
                ps = evac(r, use0 + n)
                act.activation(hT[:, ft, BANK * half:BANK * half + BANK], ps, ACT.Identity,
                               bias=modc[:, ft:ft + 1], scale=modc[:, NT + ft:NT + ft + 1]).then_inc(s[done], 1)

            def evac_qk(r, ot, n):
                t, half = n // 2, n % 2
                cols = slice(BANK * half, BANK * half + BANK)
                if half == 0:
                    if t:
                        act.wait_ge(s[f"split{ot}"], val(r, f"split{ot}", 3))
                    elif ot:
                        act.wait_ge(s["split0"], val(r, "split0", 6))
                    if ot and not t:
                        act.wait_ge(s["stored0"], val(r, "stored0", 32))
                    elif not ot and not t and not isinstance(r, int):
                        act.wait_ge(s["stored1"], val(r, "stored1", 0))
                ps = evac1(r, (USE_QK0, USE_QK1)[ot] + n)
                act.activation(qk_f[:, cols], ps, ACT.Identity, bias=b_qk[:, t, ot:ot + 1])
                act.activation(qk_p[:, t, 0, cols], ps, ACT.Identity, bias=b_qk[:, t, ot:ot + 1]).then_inc(s["d1_evac"], 1)

            def evac_v(r, n):
                ps = evac1(r, USE_V + n)
                act.copy(v1[:, 2 * n:2 * n + 2, :, 0:DK],
                         ps.rearrange("p (i h d) -> p i h d", i=2, d=DK)).then_inc(s["d1_evac"], 1)

            def evac_behind(r):
                ps = evac1(r, USE_SUM)
                act.copy(suf_t[0:NB, :, 0:DK + 1],
                         ps[0:NB, 0:H * (DK + 1)].rearrange("i (h c) -> i h c", h=H)).then_inc(s["d1_evac"], 1)

            def evac_suf(r):
                ps = evac1(r, USE_SUF)
                act.copy(suf[:, :, :], ps.rearrange("p (g i) -> p g i", g=NQ)[:, :, 0:NB]).then_inc(s["d1_evac"], 1)

            def turned(g, n):
                hh = RING[n][1]
                act.copy(q_st[KROWS:KROWS + 16, g % 2, hh, :],
                         ring[n % 2][:, 0:BANK].bitcast(BF16)[KROWS:KROWS + 16, :]).then_inc(s["turned"], 1)

            def turned_early(r, n):
                if RING[n][0] == "m":
                    wait_ring(act, r, "ring_ready", n + 1)
                    turned(1, n)

            rstd_guess(0, "ln1")
            act.wait_ge(ready, 1)
            act.wait_ge(s["mod1_loaded"], 16)
            for n in range(4):
                modulate(evac1, 0, USE_HT1, n, hT1, modc1, "d1_evac")
            for n in range(4):
                evac_qk(0, 0, n)
            for n in range(4):
                evac_v(0, n)
            for n in range(4):
                evac_qk(0, 1, n)
            evac_behind(0)
            evac_suf(0)
            for n, use in enumerate(RING):
                if use[0] == "m":
                    act.wait_ge(s["ring_ready"], n + 1)
                    turned(0, n)
            for n in range(EARLY):
                turned_early(0, n)
            rstd_guess(1, "ln1")

            def row(b, last):
                def sum_copy(g, span):
                    cols = slice(*SPANS[span])
                    act.wait_ge(s["d_ready"], val(b, "d_ready", len(SPANS) * g + span + 1))
                    act.copy(r_b[:, cols], dd[:, cols]).then_inc(s["d_copied"], 1)

                def sum_log(g, span):
                    cols = slice(*SPANS[span])
                    if span == 1:
                        act.wait_ge(s["d_copied"], val(b, "d_copied", g + 1))
                    else:
                        act.wait_ge(s["d_ready"], val(b, "d_ready", len(SPANS) * g + span + 1))
                    act.activation(r_a[:, cols], (r_b if span == 1 else dd)[:, cols], ACT.Ln).then_inc(s["r_log"], 1)

                def sum_exp(g, span):
                    cols = slice(*SPANS[span])
                    act.wait_ge(s["r_log"], val(b, "r_log", len(SPANS) * g + span + 1))
                    act.activation(r_a[:, cols], r_a[:, cols], ACT.Exp, scale=-1.0).then_inc(s["r_exp"], 1)

                def sum_hi(g, span):
                    cols = slice(*SPANS[span])
                    act.wait_ge(s["r_newton"], val(b, "r_newton", 2 * (len(SPANS) * g + span) + 2))
                    act.activation(r_h[:, cols], r_b[:, cols], ACT.Copy, scale=ab[:, 0:1]).then_inc(s["r_hi"], 1)

                def sum_mid(g, span):
                    cols = slice(*SPANS[span])
                    act.wait_ge(s["r_rest"], val(b, "r_rest", len(SPANS) * g + span + 1))
                    act.activation(r_h[:, cols], r_a[:, cols], ACT.Copy, scale=ab[:, 1:2]).then_inc(s["r_mid"], 1)

                for g in range(NQ):
                    r0, r1 = ring_base(g, last)
                    used = 0 if g else EARLY
                    for u in range(NU):
                        if g == 0 and u == 7:
                            act.wait_ge(s["out_stored"], val(b, "out_stored", 16))
                        for hh in range(QH):
                            n = QH * (NU * g + u) + hh
                            while r1 > r0 and used < s_target(g, QH * u + hh):
                                if RING[used][0] == "m":
                                    wait_ring(act, b, "ring_ready", r0 + used + 1)
                                    turned(g + 1, used)
                                used += 1
                            act.wait_ge(s["st_ready"], val(b, "st_ready", n + 1))
                            act.activation(e[:, hh, BANK * u:BANK * u + BANK], st[:, BANK * (n % 2):BANK * (n % 2) + BANK],
                                           ACT.Exp, scale=DK ** -0.5).then_inc(s["e1_done"], 1)
                            for step, span in SUM_STEPS.get((u, hh), ()):
                                {"copy": sum_copy, "log": sum_log, "exp": sum_exp, "hi": sum_hi, "mid": sum_mid}[step](g, span)

                    if r1 > r0:
                        wait_ring(act, b, "ring_ready", r1)
                        turned(g + 1, RING_S - 1)

                    def second(u, pair):
                        wait_ring(act, b, *freed(r1 + 2 * u + pair, last))
                        v = e[:, 2 * pair:2 * pair + 2, BANK * u:BANK * u + BANK]
                        act.activation(v, v, ACT.Exp).then_inc(s["e2_done"], 1)

                    for u in range(NU):
                        for pair in range(2):
                            if (u, pair) == (1, 0):
                                sum_log(g, 2)
                                sum_exp(g, 2)
                            if (u, pair) == (1, 1):
                                sum_hi(g, 2)
                            if (u, pair) == (2, 1):
                                sum_mid(g, 2)
                            second(u, pair)
                        if g < len(BETWEEN) and not last and u in BETWEEN[g]:
                            use = BETWEEN[g][u]
                            if use < USE_QK0:
                                if use == USE_HT1:
                                    act.wait_ge(s["mod1_loaded"], val(b + 1, "mod1_loaded", 16))
                                modulate(evac1, b + 1, USE_HT1, use - USE_HT1, hT1, modc1, "d1_evac")
                            else:
                                evac_qk(b + 1, 0, use - USE_QK0)

                if not last:
                    evac_v(b + 1, 0)
                    evac_v(b + 1, 1)
                for half in range(2):
                    for ft in range(NT):
                        ps = evac2(b, USE_AT + NT * half + ft)
                        act.copy(hT2[:, ft, BANK * half:BANK * half + BANK], ps).then_inc(s["d2_evac"], 1)
                if not last:
                    evac_v(b + 1, 2)
                for n in range(4):
                    ps = evac2(b, USE_O + n)
                    act.copy(tok[:, 2 * n:2 * n + 2, :], ps.rearrange("p (i d) -> p i d", i=2)).then_inc(s["d2_evac"], 1)
                if not last:
                    evac_v(b + 1, 3)
                rstd_guess(b, "ln2")
                if not last:
                    for n in range(2):
                        evac_qk(b + 1, 1, n)
                act.wait_ge(s["mod2_loaded"], val(b, "mod2_loaded", 32))
                for n in range(4):
                    modulate(evac2, b, USE_HT2, n, hT2, modc2, "d2_evac")
                if not last:
                    for n in range(2, 4):
                        evac_qk(b + 1, 1, n)
                early = 0
                for half in range(2):
                    for f in range(NF):
                        ps = evac2(b, USE_F1[half] + f)
                        act.activation(gT(f)[:, BANK * half:BANK * half + BANK], ps, ACT.Relu).then_inc(s["d2_evac"], 1)
                        if half and not last:
                            for _ in range(EARLY_AT.get(f, 0)):
                                turned_early(b + 1, early)
                                early += 1
                    if half and not last:
                        for n in range(early, EARLY):
                            turned_early(b + 1, n)
                    if not half and not last:
                        rstd_guess(b + 2, "ln1")
                        evac_behind(b + 1)
                    for n in range(2 * half, 2 * half + 2):
                        ps = evac2(b, USE_F2[half] + n % 2)
                        act.activation(n1[:, n, :], ps, ACT.Copy, scale=-1.0).then_inc(s["d2_evac"], 1)
                        if n == 0 and not last:
                            evac_suf(b + 1)

            rows(act, row)

        @block.vector
        def _(dve):
            dve.wait_ge(mod_step, 1)
            dve.tensor_scalar(c_e, c_e, 1.0, None, ALU.add).then_inc(mod_step, 1)
            dve.wait_ge(mod_step, 2)
            dve.reciprocal(c_s, c_e).then_inc(mod_own, 1)
            dve.wait_ge(mod_own, 1)
            dve.tensor_tensor(c_s, c_s, c_T, ALU.mult).then_inc(mod_step, 1)
            dve.wait_ge(consts_in, 48)
            dve.tensor_copy(id_f[:, :], c_sb[:, C_ID:C_ID + P])
            dve.tensor_copy(id_b[:, :], c_sb[:, C_ID:C_ID + P])
            dve.tensor_copy(mask_q[:, :], c_sb[:, C_MQ:C_MQ + P])
            dve.tensor_copy(mask_t[:, :], c_sb[:, C_MT:C_MT + P])
            dve.tensor_copy(sel[:, :], c_sb[:, C_SEL:C_SEL + QH * NB])
            dve.tensor_copy(d_ones[:, :, :], c_sb[:, C_DS:C_DS + 32 * NB].rearrange("p (j c) -> p j c", c=32))
            dve.tensor_copy(u_ind[:, :, :], c_sb[:, C_U:C_U + NB * NB].rearrange("p (j c) -> p j c", c=NB))
            dve.tensor_copy(seed_a[:, :], c_sb[:, C_SA:C_SA + P])
            dve.tensor_copy(seed_b[:, :], c_sb[:, C_OH:C_OH + S])
            dve.tensor_copy(ab[:, :], c_sb[:, C_AB:C_AB + 2])
            dve.memset(eps[:, :], EPS)
            dve.memset(q_st[KROWS:P, :, :, :], 0.0)
            dve.memset(negmax[:, :, :], 0.0)
            dve.memset(tok[:, 0:2, :], 0.0)
            for par in range(2):
                for hh in range(QH):
                    dve.tensor_copy(k_st[KROWS:P, par, hh, :], c_sb[KROWS:P, C_OH:C_OH + S])
            dve.memset(v1[:, :, :, DK + 1:VW], 0.0)
            dve.memset(v1[:, :, :, DK:DK + 1], 1.0)
            dve.wait_ge(s_modmm, 1)
            for n in range(3):
                dve.tensor_copy(mod_sb[:, BANK * n:BANK * n + BANK], bank1(USE_V + n)[0:B, :]).then_inc(mod_own, 1)
            dve.wait_ge(mod_own, 4)
            g_v = mod_sb.rearrange("b (a c n) -> b a c n", a=2, c=3)
            gt = mod_t.rearrange("b (a n) -> b a n", a=2)
            ga = mod_u.rearrange("b (a n) -> b a n", a=2)
            dve.tensor_scalar(gt, g_v[:, :, 2, :], 0.0, 2.0, ALU.is_ge, ALU.mult).then_inc(mod_own, 1)
            dve.scalar_tensor_tensor(out=ga, in0=g_v[:, :, 2, :], scalar=-1.0, in1=g_v[:, :, 2, :],
                                     op0=ALU.mult, op1=ALU.max).then_inc(mod_own, 1)
            dve.tensor_scalar(g_v[:, :, 1, :], g_v[:, :, 1, :], 1.0, None, ALU.add).then_inc(mod_own, 1)
            dve.wait_ge(mod_own, 7)
            dve.tensor_scalar(ga, ga, 0.25, None, ALU.max).then_inc(mod_own, 1)
            dve.wait_ge(mod_own, 8)
            dve.scalar_tensor_tensor(out=g_v[:, :, 2, :], in0=gt, scalar=-1.0, in1=ga,
                                     op0=ALU.add, op1=ALU.mult).then_inc(mod_step, 6)
            def norm(r, ln, src, dst):
                normed = {"ln1": "xn1_ready", "ln2": "xn2_ready"}[ln]
                for i in range(NB):
                    if ln == "ln2":
                        dve.wait_ge(s["x2_ready"], val(r, "x2_ready", i // 2 + 1))
                    ins = dve.bn_stats(stats[:, i, :], src[:, i, :])
                ins.then_inc(s[ln + "_stats"], 1)
                dve.wait_ge(s[ln + "_stats"], val(r, ln + "_stats", 1))
                dve.memset(ln_b[:, :], 0.0)
                for i in range(NB):
                    ins = dve.bn_aggr(mv[:, i, :], stats[:, i, :])
                ins.then_inc(s[ln + "_aggr"], 1)

                def apply():
                    newton = s[ln + "_newton"]
                    dve.wait_ge(s[ln + "_aggr"], val(r, ln + "_aggr", 1))
                    dve.wait_ge(s[ln + "_exp"], val(r, ln + "_exp", 1))
                    dve.scalar_tensor_tensor(out=ln_b[:, :], in0=mv[:, :, 1], scalar=EPS, in1=rstd[:, :],
                                             op0=ALU.add, op1=ALU.mult).then_inc(newton, 1)
                    dve.wait_ge(newton, val(r, ln + "_newton", 1))
                    dve.tensor_tensor(ln_b[:, :], ln_b[:, :], rstd[:, :], ALU.mult).then_inc(newton, 1)
                    dve.wait_ge(newton, val(r, ln + "_newton", 2))
                    dve.tensor_scalar(ln_b[:, :], ln_b[:, :], -0.5, 1.5, ALU.mult, ALU.add).then_inc(newton, 1)
                    dve.wait_ge(newton, val(r, ln + "_newton", 3))
                    dve.tensor_tensor(rstd[:, :], ln_b[:, :], rstd[:, :], ALU.mult).then_inc(newton, 1)
                    dve.wait_ge(newton, val(r, ln + "_newton", 4))
                    for i in range(NB):
                        dve.tensor_scalar(dst[:, i, :], src[:, i, :], mv[:, i, 0:1], rstd[:, i:i + 1],
                                          ALU.subtract, ALU.mult).then_inc(s[normed], 1)

                return apply

            def split_qk(r, ot):
                for t in range(2):
                    f, p3 = qk_f[:, :], qk_p[:, t, :, :]
                    dve.wait_ge(s["d1_evac"], val(r, "d1_evac", (USE_QK0, USE_QK1)[ot] + 2 * t + 2))
                    dve.tensor_tensor(f, f, p3[:, 0, :], ALU.subtract).then_inc(s[f"split{ot}"], 1)
                    dve.wait_ge(s[f"split{ot}"], val(r, f"split{ot}", 3 * t + 1))
                    dve.tensor_copy(p3[:, 1, :], f).then_inc(s[f"split{ot}"], 1)
                    dve.wait_ge(s[f"split{ot}"], val(r, f"split{ot}", 3 * t + 2))
                    dve.tensor_tensor(p3[:, 2, :], f, p3[:, 1, :], ALU.subtract).then_inc(s[f"split{ot}"], 1)

            def maxima(b, g, n, r, prologue=False):
                kind, hh, t = RING[n]
                head = QH * g + hh
                slot = ring[r % 2]
                if kind == "m":
                    return
                before = {name: 0 for name in first} if prologue else first
                dve.wait_ge(s["ring_ready"], before["ring_ready"] + val(b, "ring_ready", r + 1))
                if t == 0 and head >= 2:
                    dve.wait_ge(s["max_lo"], val(b, "max_lo", head - 1))
                w = 8 if t < NTILE - 1 else 4
                dve.tensor_reduce(negmax[:, hh % 2, 8 * t:8 * t + w],
                                  slot[:, 0:P * w].rearrange("p (a n) -> p a n", n=P), AX_X, ALU.max,
                                  negate=True).then_inc(s["ring_free"], 1)
                if t == NTILE - 1:
                    dve.wait_ge(s["ring_free"], before["ring_free"] + val(b, "ring_free", freed(r, False)[1]))
                    dve.tensor_copy(maxp[:, hh % 2, :, 0], negmax[:, hh % 2, :]).then_inc(s["max_hi"], 1)
                    dve.wait_ge(s["max_hi"], val(b, "max_hi", head + 1))
                    dve.tensor_tensor(maxp[:, hh % 2, :, 1], negmax[:, hh % 2, :], maxp[:, hh % 2, :, 0],
                                      ALU.subtract).then_inc(s["max_lo"], 1)

            dve.wait_ge(s["xin_loaded"], 16)
            norm(0, "ln1", x_in, x_in)()
            dve.wait_ge(s["out_stored"], 16)
            dve.wait_ge(mod_step, 9)
            dve.engine_nop().then_inc(ready, 2)
            split_qk(0, 0)
            split_qk(0, 1)
            for n in range(RING_S):
                maxima(0, 0, n, n, True)
            for n in range(EARLY):
                maxima(0, 1, n, n)
            dve.wait_ge(s["xin_loaded"], 32)
            norm(1, "ln1", x_in, x_in)()

            def row(b, last):
                def evac_products(g):
                    dve.wait_ge(s["pv_ready"], val(b, "pv_ready", g + 1))
                    for half in range(2):
                        cols = slice(BANK * half, BANK * half + BANK)
                        dve.tensor_tensor(o_t[:, cols].rearrange("p (i n) -> p i n", n=P), st[:, cols].rearrange("p (i n) -> p i n", n=P),
                                          suf[:, g, 4 * half:4 * half + 4].unsqueeze(2).to_broadcast([P, 4, P]),
                                          ALU.add).then_inc(s["pv_evac"], 1)

                def divide_outputs(g):
                    dve.wait_ge(s["ot_ready"], val(b, "ot_ready", g + 1))
                    v = dd[:, :].rearrange("p (i h c) -> p i h c", i=NB, c=VW)
                    rc = o_rcp[:, :].rearrange("p (i h) -> p i h", h=QH)
                    dve.reciprocal(rc, v[:, :, :, DK]).then_inc(s["o_rec"], 1)
                    dve.wait_ge(s["o_rec"], val(b, "o_rec", g + 1))
                    dve.tensor_tensor(tok[:, :, QH * DK * g:QH * DK * (g + 1)].rearrange("p i (h d) -> p i h d", d=DK),
                                      v[:, :, :, 0:DK], rc.unsqueeze(3).to_broadcast([P, NB, QH, DK]),
                                      ALU.mult).then_inc(s["o_norm"], 1)

                def invert(g, span):
                    cols = slice(*SPANS[span])
                    n = len(SPANS) * g + span
                    dve.wait_ge(s["r_exp"], val(b, "r_exp", n + 1))
                    dve.tensor_tensor(r_b[:, cols], (r_b if span == 1 else dd)[:, cols], r_a[:, cols], ALU.mult).then_inc(s["r_newton"], 1)
                    dve.wait_ge(s["r_newton"], val(b, "r_newton", 2 * n + 1))
                    dve.scalar_tensor_tensor(out=r_b[:, cols], in0=r_b[:, cols], scalar=2.0, in1=r_a[:, cols],
                                             op0=ALU.subtract, op1=ALU.mult).then_inc(s["r_newton"], 1)

                for g in range(NQ):
                    r0, r1 = ring_base(g, last)
                    used = 0 if g else EARLY
                    for u in range(NU):
                        if r1 > r0:
                            while used < s_target(g, QH * u + QH - 1):
                                maxima(b, g + 1, used, r0 + used)
                                used += 1
                        if u == 1 and g:
                            divide_outputs(g - 1)
                        if u in INVERT:
                            invert(g, INVERT[u])
                    for u in range(NU):
                        for pair in range(2):
                            if (u, pair) == (2, 0):
                                invert(g, 2)
                            r = r1 + 2 * u + pair
                            wait_ring(dve, b, "ring_ready", r + 1)
                            v = e[:, 2 * pair:2 * pair + 2, BANK * u:BANK * u + BANK]
                            dve.tensor_tensor(v, ring[r % 2][:, :].rearrange("p (i n) -> p i n", i=2), v,
                                              ALU.mult).then_inc(s["ring_free"], 1)
                    evac_products(g)
                divide_outputs(NQ - 1)

                for n in range(4):
                    t2 = tok[:, 2 * n:2 * n + 2, :]
                    dve.wait_ge(s["d2_evac"], val(b, "d2_evac", USE_O + n + 1))
                    if n == 0:
                        dve.wait_ge(s["mod2_loaded"], val(b, "mod2_loaded", 32))
                    dve.tensor_tensor(t2, t2, gates[:, 0:1, :].to_broadcast([P, 2, D]), ALU.mult).then_inc(s["ao"], 1)
                    if n == 0:
                        dve.wait_ge(s["xres_ready"], val(b, "xres_ready", 3))
                    dve.wait_ge(s["ao"], val(b, "ao", n + 1))
                    dve.tensor_tensor(x_res[:, 2 * n:2 * n + 2, :], x_res[:, 2 * n:2 * n + 2, :], t2, ALU.add).then_inc(s["x2_ready"], 1)
                norm(b, "ln2", x_res, tok)()
                if not last:
                    split_qk(b + 1, 1)
                    dve.wait_ge(s["xin_loaded"], val(b + 2, "xin_loaded", 16))
                    norm(b + 2, "ln1", x_in, x_in)()

                for n in range(4):
                    if n == 2 and not last:
                        for k in range(EARLY):
                            maxima(b + 1, 1, k, k)
                    cols = slice(BANK * (n % 2), BANK * (n % 2) + BANK)
                    y, a = n1[:, n, :], acc[:, n, :]
                    dve.wait_ge(s["d2_evac"], val(b, "d2_evac", USE_F2[n // 2] + n % 2 + 1))
                    dve.tensor_scalar(a, y, -1.0, None, ALU.is_lt).then_inc(s["lif"], 1)
                    mem, k = y, 13 * n
                    for _ in range(4):
                        dve.scalar_tensor_tensor(out=lin[:, cols], in0=mem, scalar=0.9, in1=y,
                                                 op0=ALU.mult, op1=ALU.add).then_inc(s["lif"], 1)
                        dve.wait_ge(s["lif"], val(b, "lif", k + 2))
                        dve.scalar_tensor_tensor(out=neg[:, cols], in0=mem, scalar=-1.0, in1=lin[:, cols],
                                                 op0=ALU.is_lt, op1=ALU.add).then_inc(s["lif"], 1)
                        mem = neg[:, cols]
                        dve.wait_ge(s["lif"], val(b, "lif", k + 3))
                        dve.scalar_tensor_tensor(out=a, in0=mem, scalar=-1.0, in1=a,
                                                 op0=ALU.is_lt, op1=ALU.add).then_inc(s["lif"], 1)
                        k += 3

            rows(dve, row)

        @block.gpsimd
        def _(pool):
            pool.wait_ge(ready, 1)
            pool.wait_ge(weights_in, 128)
            def bias_v(r):
                pool.wait_ge(s["d1_evac"], val(r, "d1_evac", USE_V + 4))
                bb = b_v[:, :].rearrange("p (h d) -> p h d", d=DK)
                for i in range(NB):
                    vv = v1[:, i, :, 0:DK]
                    ins = pool.tensor_tensor(vv, vv, bb, ALU.add)
                ins.then_inc(s["v_ready"], 1)

            def split_qk(r):
                for t in range(2):
                    f, p3 = qk_f[:, :], qk_p[:, t, :, :]
                    pool.wait_ge(s["d1_evac"], val(r, "d1_evac", USE_QK0 + 2 * t + 2))
                    pool.tensor_tensor(p3[:, 1, :], f, p3[:, 0, :], ALU.subtract).then_inc(s["split0"], 1)
                    pool.wait_ge(s["split0"], val(r, "split0", 3 * t + 1))
                    pool.tensor_tensor(f, f, p3[:, 0, :], ALU.subtract).then_inc(s["split0"], 1)
                    pool.wait_ge(s["split0"], val(r, "split0", 3 * t + 2))
                    pool.tensor_tensor(p3[:, 2, :], f, p3[:, 1, :], ALU.subtract).then_inc(s["split0"], 1)

            bias_v(0)

            def row(b, last):
                def split_inverses(g):
                    for span, cols in enumerate(SPANS):
                        cols = slice(*cols)
                        n = len(SPANS) * g + span + 1
                        pool.wait_ge(s["r_hi"], val(b, "r_hi", n))
                        pool.tensor_tensor(r_a[:, cols], r_b[:, cols], r_h[:, cols], ALU.add).then_inc(s["r_rest"], 1)
                        pool.wait_ge(s["r_mid"], val(b, "r_mid", n))
                        pool.tensor_tensor(r_p[:, cols], r_a[:, cols], r_h[:, cols], ALU.add).then_inc(s["rp_ready"], 1)

                split_inverses(0)
                pool.wait_ge(s["mod2_loaded"], val(b, "mod2_loaded", 32))
                pool.tensor_tensor(bo_g[:, :], b_o[:, :], gates[:, 0, :], ALU.mult).then_inc(s["xres_ready"], 1)
                pool.tensor_scalar(gates[:, 1, :], gates[:, 1, :], 0.2, None, ALU.mult).then_inc(s["xres_ready"], 1)
                pool.wait_ge(s["xres_loaded"], val(b, "xres_loaded", 16))
                pool.wait_ge(s["xres_ready"], val(b, "xres_ready", 2))
                pool.tensor_tensor(x_res[:, :, :], x_res[:, :, :], bo_g[:, :].unsqueeze(1).to_broadcast([P, NB, D]),
                                   ALU.add).then_inc(s["xres_ready"], 1)
                split_inverses(1)
                if not last:
                    split_qk(b + 1)
                split_inverses(2)
                split_inverses(3)
                if not last:
                    bias_v(b + 1)
                for half in range(2):
                    for f in range(NF):
                        pool.wait_ge(s["d2_evac"], val(b, "d2_evac", USE_F1[half] + f + 1))
                        v = gT(f)[:, BANK * half:BANK * half + BANK]
                        pool.tensor_tensor(v, v, v, ALU.mult).then_inc(s["sq_done"], 1)
                for n in range(4):
                    a = acc[:, n, :].rearrange("p (i d) -> p i d", i=2)
                    pool.wait_ge(s["lif"], val(b, "lif", 13 * (n + 1)))
                    pool.tensor_tensor(a, a, gates[:, 1:2, :].to_broadcast([P, 2, D]), ALU.mult).then_inc(s["fin"], 1)
                    pool.wait_ge(s["fin"], val(b, "fin", 2 * n + 1))
                    pool.tensor_tensor(a, a, x_res[:, 2 * n:2 * n + 2, :], ALU.add).then_inc(s["fin"], 1)

            rows(pool, row)


def kernel(**inputs):
    import numpy as _np
    import concourse.bacc as _bacc
    from concourse.bass_utils import run_bass_kernel_spmd as _run

    nc = _bacc.Bacc("TRN2", target_bir_lowering=False, num_devices=1)
    i = {k: _np.asarray(v) for k, v in inputs.items()}
    c = i["L0_c"]
    arrays = {
        "x": i["L0_attn_x"],
        "wqT": i["L0_attn_Wq_w"].T, "wkT": i["L0_attn_Wk_w"].T, "wvT": i["L0_attn_Wv_w"].T, "woT": i["L0_attn_Wo_w"].T,
        "bq": i["L0_attn_Wq_b"].reshape(NT, P).T, "bk": i["L0_attn_Wk_b"].reshape(NT, P).T, "bv": i["L0_attn_Wv_b"], "bo": i["L0_attn_Wo_b"],
        "wfcT": i["L0_ffn_W_fc"].T, "wprojT": i["L0_ffn_W_proj"].T,
        "cT": c.T.reshape(NT, P, B).transpose(1, 0, 2).reshape(P, NT * B),
        "wmod": i["L0_wmod"], "consts": constants(),
    }
    arrays = {f"in_{k}": _np.ascontiguousarray(v) for k, v in arrays.items()}
    args = [nc.dram_tensor(k, v.shape, F32, kind="ExternalInput").ap() for k, v in arrays.items()]
    out = nc.dram_tensor("out_0", (B, S, D), F32, kind="ExternalOutput").ap()
    build(nc, *args, out)
    r = _run(nc, [arrays], core_ids=[0])
    return r.results[0]["out_0"]
```
